# Optimizing a Trainium2 kernel written in Bass

```python
import numpy as np
import jax
import jax.numpy as jnp

def _softmax(x, axis=-1):
    return jax.nn.softmax(x, axis=axis)

def _gelu(x):
    return jax.nn.gelu(x, approximate=True)

def _silu(x):
    return jax.nn.silu(x)

def _sigmoid(x):
    return jax.nn.sigmoid(x)

def _layernorm(x, axis=-1, eps=1e-05):
    m = jnp.mean(x, axis=axis, keepdims=True)
    v = jnp.var(x, axis=axis, keepdims=True)
    return (x - m) / jnp.sqrt(v + eps)

def _scatter_add(tgt, idx, src, axis=0):
    return tgt.at[idx].add(src)

def _segment_sum(src, seg, n):
    return jax.ops.segment_sum(src, seg, n)
kernel_name = 'mk_gnn_resnorm_d1_gnn_r32_f78400'

def setup_inputs(seed: int=0):
    np.random.seed(seed)
    _w = jnp.asarray

    def _rec_inputs():
        import jax
        import jax.numpy as jnp
        _gk = jax.random.key(seed)
        x = -6.415e-05 + 1 * jax.random.normal(jax.random.fold_in(_gk, 1), (10000, 512), jnp.float32)
        src = jax.random.randint(jax.random.fold_in(_gk, 2), (5000,), 0, 10000, jnp.int32)
        dst = jnp.minimum((10000 * jax.random.uniform(jax.random.fold_in(_gk, 3), (5000,)) ** 2.0).astype(jnp.int32), 9999)
        _o = jnp.argsort(dst, stable=True)
        src = src[_o]
        dst = dst[_o]
        edge_attr_64 = 0.000279952 + 1.00013 * jax.random.normal(jax.random.fold_in(_gk, 11), (5000, 64), jnp.float32)
        return (x, src, dst, edge_attr_64)
    x, src, dst, edge_attr_64 = _rec_inputs()

    def _L0_gnn_setup():
        import jax, jax.numpy as jnp
        import numpy as np
        N_NODES = 625
        N_EDGES = 10000
        HIDDEN = 512
        EDGE_DIM = 64
        LN_EPS = 1e-05

        def mish(x):
            return x * jnp.tanh(jax.nn.softplus(x))
        key = jax.random.key(seed)
        ks = jax.random.split(key, 8)
        s = lambda fan_in: 1.0 / np.sqrt(fan_in)
        return {'x': jax.random.normal(ks[0], (N_NODES, HIDDEN), dtype=jnp.float32), 'edge_index': jax.random.randint(ks[1], (2, N_EDGES), 0, N_NODES, dtype=jnp.int64), 'edge_attr': jax.random.normal(ks[2], (N_EDGES, EDGE_DIM), dtype=jnp.float32), 'W1': jax.random.normal(ks[3], (2 * HIDDEN + EDGE_DIM, HIDDEN), dtype=jnp.float32) * s(2 * HIDDEN + EDGE_DIM), 'b1': jnp.zeros((HIDDEN,), dtype=jnp.float32), 'W2': jax.random.normal(ks[4], (HIDDEN, HIDDEN), dtype=jnp.float32) * s(HIDDEN), 'b2': jnp.zeros((HIDDEN,), dtype=jnp.float32), 'W3': jax.random.normal(ks[5], (2 * HIDDEN, HIDDEN), dtype=jnp.float32) * s(2 * HIDDEN), 'b3': jnp.zeros((HIDDEN,), dtype=jnp.float32), 'W4': jax.random.normal(ks[6], (HIDDEN, HIDDEN), dtype=jnp.float32) * s(HIDDEN), 'b4': jnp.zeros((HIDDEN,), dtype=jnp.float32), 'gamma': jnp.ones((HIDDEN,), dtype=jnp.float32), 'beta': jnp.zeros((HIDDEN,), dtype=jnp.float32)}
    _L0_gnn_all = _L0_gnn_setup()
    _L0_gnn_in = {k: v for k, v in _L0_gnn_all.items() if k in ('W1', 'b1', 'W2', 'b2', 'W3', 'b3', 'W4', 'b4', 'gamma', 'beta')}
    del _L0_gnn_all
    return {'x': x, 'src': src, 'dst': dst, 'edge_attr_64': edge_attr_64, 'L0_gnn_W1': _L0_gnn_in['W1'], 'L0_gnn_b1': _L0_gnn_in['b1'], 'L0_gnn_W2': _L0_gnn_in['W2'], 'L0_gnn_b2': _L0_gnn_in['b2'], 'L0_gnn_W3': _L0_gnn_in['W3'], 'L0_gnn_b3': _L0_gnn_in['b3'], 'L0_gnn_W4': _L0_gnn_in['W4'], 'L0_gnn_b4': _L0_gnn_in['b4'], 'L0_gnn_gamma': _L0_gnn_in['gamma'], 'L0_gnn_beta': _L0_gnn_in['beta']}

def reference(x, src, dst, edge_attr_64, L0_gnn_W1, L0_gnn_b1, L0_gnn_W2, L0_gnn_b2, L0_gnn_W3, L0_gnn_b3, L0_gnn_W4, L0_gnn_b4, L0_gnn_gamma, L0_gnn_beta):
    import jax
    import jax.numpy as jnp

    def _L0_gnn_ref(x, edge_index, edge_attr, W1, b1, W2, b2, W3, b3, W4, b4, gamma, beta):
        import jax, jax.numpy as jnp
        import numpy as np
        N_NODES = 625
        N_EDGES = 10000
        HIDDEN = 512
        EDGE_DIM = 64
        LN_EPS = 1e-05

        def mish(x):
            return x * jnp.tanh(jax.nn.softplus(x))
        src, dst = (edge_index[0], edge_index[1])
        edge_feat = jnp.concatenate([x[src], x[dst], edge_attr], axis=-1)
        h = mish(edge_feat @ W1 + b1)
        messages = mish(h @ W2 + b2)
        agg = jax.ops.segment_sum(messages, dst, num_segments=x.shape[0])
        u = mish(jnp.concatenate([x, agg], axis=-1) @ W3 + b3)
        out = u @ W4 + b4
        y = x + out
        mu = jnp.mean(y, axis=-1, keepdims=True)
        var = jnp.mean(jnp.square(y - mu), axis=-1, keepdims=True)
        return (y - mu) * jax.lax.rsqrt(var + LN_EPS) * gamma + beta
    edge_index = jnp.stack([src, dst])
    x = _layernorm(x + _L0_gnn_ref(x, edge_index, edge_attr_64, L0_gnn_W1, L0_gnn_b1, L0_gnn_W2, L0_gnn_b2, L0_gnn_W3, L0_gnn_b3, L0_gnn_W4, L0_gnn_b4, L0_gnn_gamma, L0_gnn_beta), axis=-1)
    return x

_drawn_inputs = setup_inputs


def setup_inputs(seed=0):
    import zlib

    import numpy as np

    out = dict(_drawn_inputs(seed))
    spreads = {'L0_gnn_b1': (0.0, 0.8),
     'L0_gnn_b2': (0.0, 0.597),
     'L0_gnn_b3': (0.0, 0.1),
     'L0_gnn_b4': (0.0, 0.1),
     'L0_gnn_gamma': (1.0, 0.2),
     'L0_gnn_beta': (0.0, 0.1)}
    factors = {'edge_attr_64': 3.306}
    for name, (base, spread) in spreads.items():
        noise = np.random.default_rng([zlib.crc32(name.encode()), seed]).standard_normal(out[name].shape)
        drawn = base * np.exp(spread * noise) if base else spread * noise
        out[name] = jnp.asarray(drawn.astype(out[name].dtype))
    for name, factor in factors.items():
        out[name] = (out[name] * factor).astype(out[name].dtype)
    return out
```

```python
import concourse.bass as bass
from concourse import mybir

ACT = mybir.ActivationFunctionType
ALU = mybir.AluOpType
AX = mybir.AxisListType
F32 = mybir.dt.float32
F32R = mybir.dt.float32r
I32 = mybir.dt.int32
BF16 = mybir.dt.bfloat16

P = 128
E_MAX = float(2 ** 14)
EPS = 1e-5
RING = 4


def gnn_kernel(nc, x, src, dst, edge_attr, W1, b1, W2, b2, W3, b3, W4, b4, gamma, beta, out):
    N, H = x.shape
    E, D = edge_attr.shape
    KC = H // P
    LE = 125
    ET = E // LE
    GT = 4
    NG = ET // GT
    GE = GT * LE
    XC = 2 * KC
    NB = 2 * KC
    NT = -(-N // P)
    PIECE = 8
    LAST = N - P
    PT = NT + 1
    assert LE * ET == E and NG * GT == ET and 2 * D == P and KC == GT == RING == 4 and NG >= 4

    pre = nc.dram_tensor("pre_table", (PT * P, H), F32).ap()

    start = -(-nc.sbuf_base // 64) * 64
    end = nc.sbuf_usable_end
    at = [start]

    def place(name, shape, dt, offset=None):
        size = 2 if dt == BF16 else 4
        for n in shape[1:]:
            size *= n
        if offset is None:
            offset = at[0]
            at[0] += -(-size // 32) * 32
        assert offset + size <= end, name
        return nc.alloc_sbuf_tensor_at(name, shape, dt, offset=offset).ap()

    ident = place("ident", [P, P], F32)
    below = place("below", [P, LE], F32)
    b1_col = place("b1_col", [P, KC], F32)
    b2_col = place("b2_col", [P, KC], F32)
    b3_row = place("b3_row", [P, H], F32)
    b4_row = place("b4_row", [P, H], F32)
    gamma_row = place("gamma_row", [P, H], F32)
    beta_row = place("beta_row", [P, H], F32)
    src_all = place("src_all", [P, ET], I32)
    dst_all = place("dst_all", [P, ET], I32)
    dst_pad = place("dst_pad", [P, ET], I32)
    dst_f = place("dst_f", [P, ET], F32)
    unread_i = place("unread_i", [P, 1], I32)
    unread_f = place("unread_f", [P, 1], F32)
    src_now = place("src_now", [P, GT], I32)
    dst_now = place("dst_now", [P, GT], I32)
    dst_sum = place("dst_sum", [P, GT], F32)
    n_before = place("n_before", [P, GT], F32)
    to_unread = place("to_unread", [P, GT], F32)
    add_row = place("add_row", [P, GT], I32)
    minus_half = place("minus_half", [P, 1], F32)
    sum1, nmean1, ssq1, var1, rstd1 = (place(k + "1", [P, RING], F32) for k in ("sum", "nmean", "ssq", "var", "rstd"))
    sum2, nmean2, ssq2, var2, rstd2 = (place(k + "2", [P, RING], F32) for k in ("sum", "nmean", "ssq", "var", "rstd"))
    shift2 = place("shift2", [P, RING], F32)
    e_buf = place("e_buf", [P, 2, H], F32)
    n_buf = place("n_buf", [P, 2, H], F32)
    f_buf = place("f_buf", [P, 2, H], F32)
    w2 = [place(f"w2_{s}", [P, KC, H], F32R) for s in ("hi", "lo")]
    w3b = [place(f"w3b_{s}", [P, KC, H], F32R) for s in ("hi", "lo")]
    at_w1 = at[0]
    w1 = [place(f"w1_{s}", [P, XC, H], F32R) for s in ("hi", "lo")]
    w1e = [place(f"w1e_{s}", [P, H], F32R) for s in ("hi", "lo")]
    at_ft = at[0]
    ft = [place(f"ft_{s}", [P, XC, GE], F32R) for s in ("hi", "lo")]
    eat = place("eat", [P, GE], F32R)
    at_xg = at[0]
    xg = place("xg", [P, 2 * GT, H], F32)
    at_h = at[0]
    ht = [place(f"ht_{s}", [P, KC, GE], F32R) for s in ("hi", "lo")]
    mt = [place(f"mt_{s}", [P, KC, GE], F32R) for s in ("hi", "lo")]
    same = place("same", [P, GT, LE], F32R)
    same_below = place("same_below", [P, GT, LE], F32)
    at_ea = at[0]
    ea_cat = place("ea_cat", [P, GT, P], F32R)
    at_z = at[0]
    zs = [place(f"z_{s}", [P, 2, H], F32R) for s in ("hi", "lo")]
    agg = place("agg", [P, GT, H], F32)
    ea_all = place("ea_all", [P, ET, D], F32)
    at_end = at[0]

    w1_in = place("w1_in", [P, XC, H], F32, at_h)
    w2_in = place("w2_in", [P, KC, H], F32, at_h + XC * H * 4)
    w3b_in = place("w3b_in", [P, KC, H], F32, at_h + (XC + KC) * H * 4)
    w1e_in = place("w1e_in", [P, H], F32, at_z)
    assert at_h + (XC + 2 * KC) * H * 4 <= at_ea

    w3a = [place(f"w3a_{s}", [P, KC, H], F32R, at_w1 + i * KC * H * 4) for i, s in enumerate(("hi", "lo"))]
    w4 = [place(f"w4_{s}", [P, KC, H], F32R, at_w1 + (2 + i) * KC * H * 4) for i, s in enumerate(("hi", "lo"))]
    w34_in = place("w34_in", [P, 2 * KC, H], F32, at_xg)
    at[0] = at_ft
    xt = [place(f"xt_{s}", [P, 2, KC, P], F32R) for s in ("hi", "lo")]
    ut = [place(f"ut_{s}", [P, 2, KC, P], F32R) for s in ("hi", "lo")]
    x_row = place("x_row", [P, RING, H], F32)
    y_row = place("y_row", [P, RING, H], F32)
    assert at[0] <= at_xg
    at[0] = at_h
    xb_row = place("xb_row", [P, RING, H], F32)
    w_row = place("w_row", [P, 2, H], F32)
    v_row = place("v_row", [P, RING, H], F32)
    o_row = place("o_row", [P, RING, H], F32)
    unused = place("unused", [P, 2, H], BF16)
    assert at[0] <= at_end

    ps = nc.alloc_psum_tensor("ps", [P, 8, H], F32).ap()
    BLOCK, TURN, ROWS = 0, 4, 6

    pads_set = nc.alloc_semaphore("pads_set")
    loaded_src = nc.alloc_semaphore("loaded_src")
    loaded_dst = nc.alloc_semaphore("loaded_dst")
    loaded_pad = nc.alloc_semaphore("loaded_pad")
    loaded_ea = nc.alloc_semaphore("loaded_ea")
    loaded_w1a = nc.alloc_semaphore("loaded_w1a")
    loaded_w1b = nc.alloc_semaphore("loaded_w1b")
    loaded_w1e = nc.alloc_semaphore("loaded_w1e")
    loaded_w2 = nc.alloc_semaphore("loaded_w2")
    loaded_w3b = nc.alloc_semaphore("loaded_w3b")
    loaded_w3a = nc.alloc_semaphore("loaded_w3a")
    loaded_w4 = nc.alloc_semaphore("loaded_w4")
    loaded_bias = nc.alloc_semaphore("loaded_bias")
    loaded_b3 = nc.alloc_semaphore("loaded_b3")
    loaded_rows = nc.alloc_semaphore("loaded_rows")
    constants_made = nc.alloc_semaphore("constants_made")
    unread_set = nc.alloc_semaphore("unread_set")
    dst_float = nc.alloc_semaphore("dst_float")
    w_hi_ready = nc.alloc_semaphore("w_hi_ready")
    w_split = nc.alloc_semaphore("w_split")
    table_ready = nc.alloc_semaphore("table_ready")
    added = nc.alloc_semaphore("added")
    src_staged = nc.alloc_semaphore("src_staged")
    dst_staged = nc.alloc_semaphore("dst_staged")
    turned_x = nc.alloc_semaphore("turned_x")
    ft_hi_ready = nc.alloc_semaphore("ft_hi_ready")
    ft_split = nc.alloc_semaphore("ft_split")
    ea_hi_ready = nc.alloc_semaphore("ea_hi_ready")
    ea_cat_ready = nc.alloc_semaphore("ea_cat_ready")
    turned_ea = nc.alloc_semaphore("turned_ea")
    eat_ready = nc.alloc_semaphore("eat_ready")
    block_done = nc.alloc_semaphore("block_done")
    e_ready = nc.alloc_semaphore("e_ready")
    e_held = nc.alloc_semaphore("e_held")
    n_ready = nc.alloc_semaphore("n_ready")
    ln_done = nc.alloc_semaphore("ln_done")
    inv_ready = nc.alloc_semaphore("inv_ready")
    vn_ready = nc.alloc_semaphore("vn_ready")
    mish_ready = nc.alloc_semaphore("mish_ready")
    mish_hi_ready = nc.alloc_semaphore("mish_hi_ready")
    mish_split = nc.alloc_semaphore("mish_split")
    z_done = nc.alloc_semaphore("z_done")
    z_hi_ready = nc.alloc_semaphore("z_hi_ready")
    z_split = nc.alloc_semaphore("z_split")
    sum_done = nc.alloc_semaphore("sum_done")
    agg_ready = nc.alloc_semaphore("agg_ready")
    dst_sum_ready = nc.alloc_semaphore("dst_sum_ready")
    turned_dst = nc.alloc_semaphore("turned_dst")
    same_part_ready = nc.alloc_semaphore("same_part_ready")
    same_ready = nc.alloc_semaphore("same_ready")
    counted = nc.alloc_semaphore("counted")
    distance = nc.alloc_semaphore("distance")
    moved = nc.alloc_semaphore("moved")
    add_row_ready = nc.alloc_semaphore("add_row_ready")
    turned_node = nc.alloc_semaphore("turned_node")
    xt_hi_ready = nc.alloc_semaphore("xt_hi_ready")
    xt_split = nc.alloc_semaphore("xt_split")
    w3_done = nc.alloc_semaphore("w3_done")
    v_ready = nc.alloc_semaphore("v_ready")
    turned_u = nc.alloc_semaphore("turned_u")
    ut_hi_ready = nc.alloc_semaphore("ut_hi_ready")
    ut_split = nc.alloc_semaphore("ut_split")
    w4_done = nc.alloc_semaphore("w4_done")
    x_b4 = nc.alloc_semaphore("x_b4")
    x_beta = nc.alloc_semaphore("x_beta")
    y_ready = nc.alloc_semaphore("y_ready")
    nmean1_ready = nc.alloc_semaphore("nmean1_ready")
    squared1 = nc.alloc_semaphore("squared1")
    var1_ready = nc.alloc_semaphore("var1_ready")
    rstd1_ready = nc.alloc_semaphore("rstd1_ready")
    y_gamma_ready = nc.alloc_semaphore("y_gamma_ready")
    w_ready = nc.alloc_semaphore("w_ready")
    nmean2_ready = nc.alloc_semaphore("nmean2_ready")
    squared2 = nc.alloc_semaphore("squared2")
    var2_ready = nc.alloc_semaphore("var2_ready")
    rstd2_ready = nc.alloc_semaphore("rstd2_ready")
    shift2_ready = nc.alloc_semaphore("shift2_ready")
    normed = nc.alloc_semaphore("normed")
    src_in = [nc.alloc_semaphore(f"src_in{j}") for j in range(GT)]
    dst_in = [nc.alloc_semaphore(f"dst_in{j}") for j in range(GT)]
    x_in = [nc.alloc_semaphore(f"x_in{j}") for j in range(RING)]
    pre_in = [nc.alloc_semaphore(f"pre_in{j}") for j in range(RING)]
    stored = [nc.alloc_semaphore(f"stored{j}") for j in range(RING)]

    def past(count):
        return not isinstance(count, int) or count > 0

    def split_matmul(pe, out_, lhs, rhs, first, last):
        pe.matmul(out_, lhs[0], rhs[0], start=first, stop=False)
        pe.matmul(out_, lhs[0], rhs[1], start=False, stop=False)
        return pe.matmul(out_, lhs[1], rhs[0], start=False, stop=last)

    def run_steps(eng, step, begin, stop=None):
        first, end = 3, (NT - 2 - 3 - (RING - 1)) // RING + 1
        inside = lambda a, k: 0 <= a + k < NT
        for k in range(begin, stop or RING * first):
            step(0, 0, k, inside)
        if stop:
            return
        with eng.Fori(first, end) as b:
            for k in range(RING):
                step(RING * b, b, k, lambda a, k: True)
        for k in range(RING * end, NT + 6):
            step(0, 0, k, inside)

    with nc.Block() as block:

        @block.sync
        def _(sp):
            def row(v):
                return v.rearrange("(a d) -> a d", a=1).to_broadcast([P, H])

            sp.wait_ge(pads_set, 3)
            sp.dma_start(src_all[0:LE, :], src.rearrange("(p t) -> p t", t=ET)).then_inc(loaded_src, 16)
            sp.dma_start(dst_all[0:LE, :], dst.rearrange("(p t) -> p t", t=ET)).then_inc(loaded_dst, 16)
            sp.dma_start(dst_pad[0:LE, :], dst.rearrange("(p t) -> p t", t=ET)).then_inc(loaded_pad, 16)
            sp.dma_start(ea_all[0:LE], edge_attr.rearrange("(p t) d -> p t d", t=ET)).then_inc(loaded_ea, 16)
            half = XC // 2
            for i, loaded in enumerate((loaded_w1a, loaded_w1b)):
                sp.dma_start(w1_in[:, i * half:(i + 1) * half, :],
                             W1[i * H:(i + 1) * H, :].rearrange("(c p) n -> p c n", p=P)).then_inc(loaded, 16)
            for i in range(2):
                sp.dma_start(w1e_in[i * D:(i + 1) * D, :], W1[2 * H:2 * H + D, :]).then_inc(loaded_w1e, 16)
            sp.dma_start(w2_in, W2.rearrange("(c p) n -> p c n", p=P)).then_inc(loaded_w2, 16)
            sp.dma_start(w3b_in, W3[H:2 * H, :].rearrange("(c p) n -> p c n", p=P)).then_inc(loaded_w3b, 16)
            sp.dma_start(b1_col, b1.rearrange("(c p) -> p c", p=P),
                         allow_slow_non_contiguous=True).then_inc(loaded_bias, 16)
            sp.dma_start(b2_col, b2.rearrange("(c p) -> p c", p=P),
                         allow_slow_non_contiguous=True).then_inc(loaded_bias, 16)
            sp.dma_start(b3_row, row(b3)).then_inc(loaded_b3, 16)
            sp.wait_ge(loaded_b3, 16)
            for j in range(GT):
                sp.wait_ge(dst_in[j], 32)
            for t in range(0, PT, PIECE):
                n = min(PIECE, PT - t)
                if past(16 * (t // PIECE)):
                    sp.wait_ge(table_ready, 16 * (t // PIECE))
                sp.dma_start(pre[t * P:(t + n) * P, :].rearrange("(n p) d -> p n d", p=P),
                             b3_row.rearrange("p (a d) -> p a d", a=1).to_broadcast([P, n, H])
                             ).then_inc(table_ready, 16)
            for tile_, v in ((b4_row, b4), (gamma_row, gamma), (beta_row, beta)):
                sp.dma_start(tile_, row(v)).then_inc(loaded_rows, 16)

            sp.wait_ge(turned_x, XC * NG)
            sp.dma_start(w34_in[:, 0:KC, :], W3[0:H, :].rearrange("(c p) n -> p c n", p=P)).then_inc(loaded_w3a, 16)
            sp.dma_start(w34_in[:, KC:2 * KC, :], W4.rearrange("(c p) n -> p c n", p=P)).then_inc(loaded_w4, 16)
            if past(NB * (NG - 1) + KC):
                sp.wait_ge(block_done, NB * (NG - 1) + KC)

            def rows_of(a, b, k):
                t = a + k
                return slice(LAST, LAST + P) if isinstance(t, int) and t == NT - 1 else bass.ds(t * P, P)

            def load_x(a, b, k):
                if past(a + k - RING + 1):
                    sp.wait_ge(turned_node, a + k - RING + 1)
                if past(a + k - RING + 1):
                    sp.wait_ge(x_beta, a + k - RING + 1)
                sp.dma_start(x_row[:, k % RING, :], x[rows_of(a, b, k), :]).then_inc(x_in[k % RING], 16)

            def load_pre(a, b, k):
                sp.wait_ge(mish_ready, NB * NG + a + k - RING + 1)
                sp.dma_start(v_row[:, k % RING, :], pre[rows_of(a, b, k), :]).then_inc(pre_in[k % RING], 16)

            def store(a, b, k):
                sp.wait_ge(normed, a + k + 1)
                t = a + k
                if isinstance(t, int) and t == NT - 1:
                    skip = NT * P - N
                    sp.dma_start(out[LAST + skip:N, :], o_row[skip:P, k % RING, :]).then_inc(stored[k % RING], 16)
                else:
                    sp.dma_start(out[bass.ds(t * P, P), :], o_row[:, k % RING, :]).then_inc(stored[k % RING], 16)

            def step(a, b, k, live):
                if live(a, k + 3):
                    load_x(a, b, k + 3)
                if live(a, k + 2):
                    load_pre(a, b, k + 2)
                if live(a, k - 6):
                    store(a, b, k - 6)

            for k in range(3):
                load_x(0, 0, k)
            sp.wait_ge(added, 16 * ET)
            for k in range(2):
                load_pre(0, 0, k)
            run_steps(sp, step, 0)
            for j in range(RING):
                sp.wait_ge(stored[j], 16 * len(range(j, NT, RING)))

        @block.gpsimd
        def _(pool):
            pool.memset(src_all, 0).then_inc(pads_set, 1)
            pool.memset(dst_all, 0).then_inc(pads_set, 1)
            pool.iota(unread_i, [[0, 1]], base=NT * P, channel_multiplier=1).then_inc(unread_set, 1)
            pool.iota(dst_pad, [[0, ET]], base=NT * P, channel_multiplier=1).then_inc(pads_set, 1)

            def to_count(count):
                return count if isinstance(count, int) else pool.to_reg(count)


            def gather_src(g):
                if past(XC * (g - 1) + KC):
                    pool.wait_ge(turned_x, XC * (g - 1) + KC)
                pool.tensor_copy(src_now, src_all[:, bass.ds(g * GT, GT)]).then_inc(src_staged, 1)
                staged = to_count(g + 1)
                pool.wait_ge(pads_set, 3)
                pool.wait_ge(src_staged, staged)
                for j in range(GT):
                    pool.indirect_dma_start(
                        out=xg[:, j, :], out_offset=None, in_=x,
                        in_offset=bass.IndirectOffsetOnAxis(ap=src_now[:, j:j + 1], axis=0),
                    ).then_inc(src_in[j], 16)

            def gather_dst(g):
                if past(XC * g):
                    pool.wait_ge(turned_x, XC * g)
                pool.tensor_copy(dst_now, dst_all[:, bass.ds(g * GT, GT)]).then_inc(dst_staged, 1)
                staged = to_count(g + 1)
                pool.wait_ge(pads_set, 3)
                pool.wait_ge(dst_staged, staged)
                for j in range(GT):
                    pool.indirect_dma_start(
                        out=xg[:, GT + j, :], out_offset=None, in_=x,
                        in_offset=bass.IndirectOffsetOnAxis(ap=dst_now[:, j:j + 1], axis=0),
                    ).then_inc(dst_in[j], 16)

            def add_rows(g, j):
                chosen, summed, before = to_count(g + 1), to_count(GT * g + j + 1), to_count(16 * (GT * g + j))
                pool.wait_ge(pads_set, 3)
                pool.wait_ge(add_row_ready, chosen)
                pool.wait_ge(agg_ready, summed)
                if past(before):
                    pool.wait_ge(added, before)
                pool.indirect_dma_start(
                    out=pre, out_offset=bass.IndirectOffsetOnAxis(ap=add_row[:, j:j + 1], axis=0),
                    in_=agg[:, j, :], in_offset=None, compute_op=ALU.add,
                ).then_inc(added, 16)

            def group(g, first=False, last=False, over=False):
                if not first:
                    add_rows(g - 1, 0)
                if not last and not over:
                    gather_src(g + 2)
                if not first:
                    add_rows(g - 1, 1)
                    add_rows(g - 1, 2)
                if not last and not over:
                    gather_dst(g + 2)
                if not first:
                    add_rows(g - 1, 3)

            pool.wait_ge(pads_set, 3)
            pool.wait_ge(loaded_src, 16)
            gather_src(0)
            pool.wait_ge(loaded_dst, 16)
            gather_dst(0)
            pool.memset(ident, 0.0).then_inc(constants_made, 1)
            pool.memset(below, 1.0).then_inc(constants_made, 1)
            pool.memset(minus_half, -0.5).then_inc(constants_made, 1)
            pool.memset(n_before, 0.0).then_inc(constants_made, 1)
            pool.memset(agg, 0.0).then_inc(constants_made, 1)
            pool.wait_ge(constants_made, 5)
            pool.affine_select(out=ident, in_=ident, compare_op=ALU.not_equal, fill=1.0, base=0,
                               pattern=[[-1, P]], channel_multiplier=1).then_inc(constants_made, 1)
            pool.affine_select(out=below, in_=below, compare_op=ALU.is_gt, fill=0.0, base=0,
                               pattern=[[-1, LE]], channel_multiplier=1).then_inc(constants_made, 1)
            gather_src(1)
            gather_dst(1)
            group(0, first=True)
            pool.wait_ge(table_ready, 16 * len(range(0, PT, PIECE)))
            group(1)
            with pool.Fori(2, NG - 2) as g:
                group(g)
            group(NG - 2, last=True)
            group(NG - 1, last=True)
            group(NG, over=True)

            pool.wait_ge(loaded_rows, 48)

            def step(a, b, k, live):
                t1, t2 = k - 3, k - 4
                q, q1, q2 = (slice(t % RING, t % RING + 1) for t in (k, t1, t2))
                if live(a, t2):
                    count = to_count(a + t2 + 1)
                    pool.wait_ge(pads_set, 3)
                    pool.wait_ge(w_ready, count)
                    pool.tensor_scalar(nmean2[:, q2], sum2[:, q2], -1.0 / H, 0.0, ALU.mult, ALU.add).then_inc(nmean2_ready, 1)
                if live(a, k):
                    pool.wait_ge(x_in[k % RING], 16 * (b + k // RING + 1))
                    if past(a + k - RING + 1):
                        pool.wait_ge(w_ready, a + k - RING + 1)
                    pool.tensor_tensor(y_row[:, k % RING, :], x_row[:, k % RING, :], b4_row, ALU.add).then_inc(x_b4, 1)
                if live(a, t1):
                    count = to_count(a + t1 + 1)
                    pool.wait_ge(pads_set, 3)
                    pool.wait_ge(y_ready, count)
                    pool.tensor_scalar(nmean1[:, q1], sum1[:, q1], -1.0 / H, 0.0, ALU.mult, ALU.add).then_inc(nmean1_ready, 1)
                if live(a, t2):
                    count = to_count(a + t2 + 1)
                    pool.wait_ge(pads_set, 3)
                    pool.wait_ge(squared2, count)
                    pool.tensor_scalar(var2[:, q2], ssq2[:, q2], 1.0 / H, EPS, ALU.mult, ALU.add).then_inc(var2_ready, 1)
                    pool.wait_ge(var2_ready, a + t2 + 1)
                    pool.tensor_tensor(rstd2[:, q2], var2[:, q2], minus_half, ALU.pow).then_inc(rstd2_ready, 1)
                    pool.wait_ge(nmean2_ready, a + t2 + 1)
                    pool.wait_ge(rstd2_ready, a + t2 + 1)
                    pool.tensor_tensor(shift2[:, q2], rstd2[:, q2], nmean2[:, q2], ALU.mult).then_inc(shift2_ready, 1)
                if live(a, t1):
                    count = to_count(a + t1 + 1)
                    pool.wait_ge(pads_set, 3)
                    pool.wait_ge(squared1, count)
                    pool.tensor_scalar(var1[:, q1], ssq1[:, q1], 1.0 / H, EPS, ALU.mult, ALU.add).then_inc(var1_ready, 1)
                    pool.wait_ge(var1_ready, a + t1 + 1)
                    pool.tensor_tensor(rstd1[:, q1], var1[:, q1], minus_half, ALU.pow).then_inc(rstd1_ready, 1)
                if live(a, k):
                    pool.tensor_tensor(xb_row[:, k % RING, :], x_row[:, k % RING, :], beta_row,
                                       ALU.add).then_inc(x_beta, 1)

            run_steps(pool, step, 0)

        @block.tensor
        def _(pe):
            def turn_chunk(g, c):
                first, gathered = (0, src_in) if c < KC else (GT, dst_in)
                cc = c % KC
                if c == 0:
                    if past(NB * (g - 1) + KC):
                        pe.wait_ge(block_done, NB * (g - 1) + KC)
                if c == 0:
                    if past(g):
                        pe.wait_ge(eat_ready, g)
                elif c == 1:
                    if past(g - 1):
                        pe.wait_ge(same_ready, g - 1)
                    if past(XC * g):
                        pe.wait_ge(ft_split, XC * g)
                else:
                    if past(XC * g + c - 1):
                        pe.wait_ge(ft_split, XC * g + c - 1)
                for j in range(GT):
                    if cc == 0:
                        pe.wait_ge(gathered[j], 16 * (g + 1))
                    t = pe.transpose(ps[:, TURN + c % 2, j * LE:(j + 1) * LE],
                                     xg[0:LE, first + j, cc * P:(cc + 1) * P], ident[0:LE, 0:LE])
                t.then_inc(turned_x, 1)

            def turn_ea(g):
                pe.wait_ge(ea_cat_ready, g + 1)
                if past(XC * g + XC - 1):
                    pe.wait_ge(ft_split, XC * g + XC - 1)
                for j in range(GT):
                    t = pe.transpose(ps[:, TURN, j * LE:(j + 1) * LE], ea_cat[0:LE, j, :].bitcast(F32),
                                     ident[0:LE, 0:LE])
                t.then_inc(turned_ea, 1)

            def turn_dst(g):
                pe.wait_ge(dst_sum_ready, g + 1)
                if isinstance(g, int) and g == NG - 1:
                    pe.wait_ge(xt_split, 2)
                else:
                    pe.wait_ge(ft_split, XC * (g + 2))
                for j in range(GT):
                    t = pe.transpose(ps[0:LE, TURN + 1, j * LE:(j + 1) * LE],
                                     dst_sum[0:LE, j:j + 1].to_broadcast([LE, LE]), ident[0:LE, 0:LE])
                t.then_inc(turned_dst, 1)

            def w1_product(g):
                for mb in range(KC):
                    cols = slice(mb * P, (mb + 1) * P)
                    o = ps[:, BLOCK + mb, 0:GE]
                    if past(NB * g + mb - KC + 1):
                        pe.wait_ge(vn_ready, NB * g + mb - KC + 1)
                    for c in range(XC):
                        if mb == 0:
                            if isinstance(g, int) and g == 0:
                                pe.wait_ge(w_split, c + 1)
                            pe.wait_ge(ft_split, XC * g + c + 1)
                        split_matmul(pe, o, [w[:, c, cols] for w in w1], [f[:, c, :] for f in ft], c == 0, False)
                    if mb == 0:
                        if isinstance(g, int) and g == 0:
                            pe.wait_ge(w_split, XC + 1)
                        pe.wait_ge(eat_ready, g + 1)
                    pe.matmul(o, w1e[0][:, cols], eat, start=False, stop=False)
                    pe.matmul(o, w1e[1][0:D, cols], eat[0:D, :], start=False, stop=True).then_inc(block_done, 1)

            def w2_product(g):
                for mb in range(KC):
                    cols = slice(mb * P, (mb + 1) * P)
                    o = ps[:, BLOCK + mb, 0:GE]
                    pe.wait_ge(vn_ready, NB * g + mb + 1)
                    for c in range(KC):
                        if mb == 0:
                            if isinstance(g, int) and g == 0:
                                pe.wait_ge(w_split, XC + 1 + c + 1)
                            pe.wait_ge(mish_split, NB * g + c + 1)
                        mm = split_matmul(pe, o, [w[:, c, cols] for w in w2], [h[:, c, :] for h in ht],
                                          c == 0, c == KC - 1)
                    mm.then_inc(block_done, 1)

            def z_tile(g, j):
                if isinstance(g, int) and g == 0 and j == 0:
                    pe.wait_ge(w_split, XC + 1 + 2 * KC)
                pe.wait_ge(mish_split, NB * (g + 1))
                if past(GT * g + j - 1):
                    pe.wait_ge(agg_ready, GT * g + j - 1)
                lanes = slice(j * LE, (j + 1) * LE)
                for c in range(KC):
                    mm = split_matmul(pe, ps[0:LE, ROWS + j % 2, :], [m[:, c, lanes] for m in mt],
                                      [w[:, c, :] for w in w3b], c == 0, c == KC - 1)
                mm.then_inc(z_done, 1)

            def sum_tile(g, j):
                pe.wait_ge(same_ready, g + 1)
                pe.wait_ge(z_split, GT * g + j + 1)
                o = ps[0:LE, ROWS + j % 2, :]
                pe.matmul(o, same[0:LE, j, :], zs[0][0:LE, j % 2, :], start=True, stop=False)
                pe.matmul(o, same[0:LE, j, :], zs[1][0:LE, j % 2, :], start=False, stop=True).then_inc(sum_done, 1)

            def group(g, first=False, last=False, over=False):
                ahead = not last and not over
                if not first:
                    turn_dst(g - 1)
                if not over:
                    w1_product(g)
                if not first:
                    z_tile(g - 1, 0)
                    z_tile(g - 1, 1)
                if ahead:
                    turn_chunk(g + 1, 0)
                    turn_chunk(g + 1, 1)
                if not first:
                    sum_tile(g - 1, 0)
                if ahead:
                    turn_chunk(g + 1, 2)
                    turn_chunk(g + 1, 3)
                if not first:
                    z_tile(g - 1, 2)
                    sum_tile(g - 1, 1)
                if ahead:
                    turn_chunk(g + 1, 4)
                    turn_chunk(g + 1, 5)
                if not first:
                    z_tile(g - 1, 3)
                    sum_tile(g - 1, 2)
                if ahead:
                    turn_chunk(g + 1, 6)
                    turn_chunk(g + 1, 7)
                    turn_ea(g + 1)
                if not first:
                    sum_tile(g - 1, 3)
                if not over:
                    w2_product(g)

            pe.wait_ge(constants_made, 7)
            for c in range(XC):
                turn_chunk(0, c)
            turn_ea(0)
            group(0, first=True)
            group(1)
            with pe.Fori(2, NG - 1) as g:
                group(g)
            group(NG - 1, last=True)

            def turn_x(a, b, k):
                pe.wait_ge(x_in[k % RING], 16 * (b + k // RING + 1))
                if past(a + k - 1):
                    pe.wait_ge(xt_split, a + k - 1)
                if isinstance(a, int) and a + k in (1, 3):
                    pe.wait_ge(same_ready, NG - 1 if a + k == 1 else NG)
                for c in range(KC):
                    t = pe.transpose(ps[:, TURN + k % 2, c * P:(c + 1) * P],
                                     x_row[:, k % RING, c * P:(c + 1) * P], ident)
                t.then_inc(turned_node, 1)

            def turn_u(a, b, k):
                pe.wait_ge(mish_ready, NB * NG + a + k + 1)
                if past(a + k - 1):
                    pe.wait_ge(ut_split, a + k - 1)
                for c in range(KC):
                    t = pe.transpose(ps[:, BLOCK + 2 + k % 2, c * P:(c + 1) * P],
                                     f_buf[:, k % 2, c * P:(c + 1) * P], ident)
                t.then_inc(turned_u, 1)

            def w3_product(a, b, k):
                if isinstance(a, int) and a + k == 0:
                    pe.wait_ge(w_split, XC + 1 + 3 * KC)
                pe.wait_ge(xt_split, a + k + 1)
                if isinstance(a, int) and a + k < 2:
                    pe.wait_ge(vn_ready, NB * NG - KC + a + k + 1)
                else:
                    if past(a + k - 1):
                        pe.wait_ge(v_ready, a + k - 1)
                for c in range(KC):
                    mm = split_matmul(pe, ps[:, BLOCK + k % 2, :], [v[:, k % 2, c, :] for v in xt],
                                      [w[:, c, :] for w in w3a], c == 0, c == KC - 1)
                mm.then_inc(w3_done, 1)

            def w4_product(a, b, k):
                if isinstance(a, int) and a + k == 0:
                    pe.wait_ge(w_split, XC + 1 + 4 * KC)
                pe.wait_ge(ut_split, a + k + 1)
                if past(a + k - 1):
                    pe.wait_ge(y_ready, a + k - 1)
                for c in range(KC):
                    mm = split_matmul(pe, ps[:, ROWS + k % 2, :], [v[:, k % 2, c, :] for v in ut],
                                      [w[:, c, :] for w in w4], c == 0, c == KC - 1)
                mm.then_inc(w4_done, 1)

            def step(a, b, k, live):
                if live(a, k + 1):
                    turn_x(a, b, k + 1)
                if live(a, k - 3):
                    w4_product(a, b, k - 3)
                if live(a, k - 2):
                    turn_u(a, b, k - 2)
                if live(a, k):
                    w3_product(a, b, k)

            pe.wait_ge(eat_ready, NG)
            turn_x(0, 0, 0)
            run_steps(pe, step, 0, 2)
            group(NG, over=True)
            pe.wait_ge(vn_ready, NB * NG)
            pe.wait_ge(agg_ready, GT * NG)
            run_steps(pe, step, 2)

        @block.scalar
        def _(act):
            def weight_hi(out_, in_):
                act.activation(out_, in_, ACT.Copy).then_inc(w_hi_ready, 1)

            def mish_exp(g, b):
                i = NB * g + b
                act.wait_ge(block_done, i + 1)
                if past(i - 1):
                    act.wait_ge(mish_ready, i - 1)
                act.activation(e_buf[:, b % 2, 0:GE], ps[:, BLOCK + b % KC, 0:GE], ACT.Exp,
                               bias=(b1_col if b < KC else b2_col)[:, b % KC:b % KC + 1]).then_inc(e_ready, 1)

            def mish_inverse(slot, width, i):
                act.wait_ge(n_ready, i + 1)
                act.activation(e_buf[:, slot, 0:width], n_buf[:, slot, 0:width], ACT.Ln, bias=2.0).then_inc(ln_done, 1)
                act.wait_ge(ln_done, i + 1)
                act.activation(e_buf[:, slot, 0:width], e_buf[:, slot, 0:width], ACT.Exp, scale=-1.0).then_inc(inv_ready, 1)

            def mish_hi(g, b):
                i = NB * g + b
                act.wait_ge(mish_ready, i + 1)
                if b < KC:
                    if past(NB * g):
                        act.wait_ge(block_done, NB * g)
                else:
                    if past(GT * g):
                        act.wait_ge(z_done, GT * g)
                act.activation((ht if b < KC else mt)[0][:, b % KC, :], f_buf[:, b % 2, 0:GE], ACT.Copy).then_inc(mish_hi_ready, 1)

            def mish_blocks(g, first_block):
                mish_exp(g, first_block)
                for b in range(first_block, first_block + KC):
                    mish_inverse(b % 2, GE, NB * g + b)
                    if b + 1 < first_block + KC:
                        mish_exp(g, b + 1)
                    mish_hi(g, b)

            def ft_hi(g, c):
                act.wait_ge(turned_x, XC * g + c + 1)
                if c == 0:
                    if past(NB * (g - 1) + KC):
                        act.wait_ge(block_done, NB * (g - 1) + KC)
                act.activation(ft[0][:, c, :], ps[:, TURN + c % 2, 0:GE], ACT.Copy).then_inc(ft_hi_ready, 1)

            def z_hi(g, j):
                act.wait_ge(z_done, GT * g + j + 1)
                if past(GT * g + j - 1):
                    act.wait_ge(sum_done, GT * g + j - 1)
                act.activation(zs[0][0:LE, j % 2, :], ps[0:LE, ROWS + j % 2, :], ACT.Copy).then_inc(z_hi_ready, 1)

            def agg_out(g, j):
                act.wait_ge(sum_done, GT * g + j + 1)
                if past(16 * (GT * (g - 1) + j + 1)):
                    act.wait_ge(added, 16 * (GT * (g - 1) + j + 1))
                act.activation(agg[0:LE, j, :], ps[0:LE, ROWS + j % 2, :], ACT.Copy).then_inc(agg_ready, 1)

            def group(g, first=False, last=False, over=False):
                ahead = not last and not over
                if not over:
                    mish_blocks(g, 0)
                if not first:
                    z_hi(g - 1, 0)
                    z_hi(g - 1, 1)
                if ahead:
                    ft_hi(g + 1, 0)
                    ft_hi(g + 1, 1)
                if not first:
                    agg_out(g - 1, 0)
                if ahead:
                    ft_hi(g + 1, 2)
                    ft_hi(g + 1, 3)
                if not first:
                    z_hi(g - 1, 2)
                    agg_out(g - 1, 1)
                if ahead:
                    ft_hi(g + 1, 4)
                    ft_hi(g + 1, 5)
                if not first:
                    z_hi(g - 1, 3)
                    agg_out(g - 1, 2)
                if ahead:
                    ft_hi(g + 1, 6)
                    ft_hi(g + 1, 7)
                if not first:
                    agg_out(g - 1, 3)
                if last:
                    act.wait_ge(loaded_w3a, 16)
                    for c in range(KC):
                        weight_hi(w3a[0][:, c, :], w34_in[:, c, :])
                    act.wait_ge(loaded_w4, 16)
                    for c in range(KC):
                        weight_hi(w4[0][:, c, :], w34_in[:, KC + c, :])
                if not over:
                    mish_blocks(g, KC)

            act.preload_act_table_set("natural_log_exp_and_others")
            for c in range(XC):
                if c == 0:
                    act.wait_ge(loaded_w1a, 16)
                elif c == KC:
                    act.wait_ge(loaded_w1b, 16)
                weight_hi(w1[0][:, c, :], w1_in[:, c, :])
                ft_hi(0, c)
            act.wait_ge(loaded_w1e, 32)
            weight_hi(w1e[0], w1e_in)
            act.wait_ge(loaded_w2, 16)
            for c in range(KC):
                weight_hi(w2[0][:, c, :], w2_in[:, c, :])
            act.wait_ge(loaded_w3b, 16)
            for c in range(KC):
                weight_hi(w3b[0][:, c, :], w3b_in[:, c, :])
            act.wait_ge(loaded_bias, 32)
            act.wait_ge(constants_made, 7)
            act.wait_ge(w_split, XC + 1 + 2 * KC)
            group(0, first=True)
            group(1)
            with act.Fori(2, NG - 1) as g:
                group(g)
            group(NG - 1, last=True)

            M0 = NB * NG

            def xt_hi(a, b, k):
                act.wait_ge(turned_node, a + k + 1)
                if past(a + k - 1):
                    act.wait_ge(w3_done, a + k - 1)
                act.activation(xt[0][:, k % 2].rearrange("p c n -> p (c n)"), ps[:, TURN + k % 2, :],
                               ACT.Copy).then_inc(xt_hi_ready, 1)

            xt_hi(0, 0, 0)
            xt_hi(0, 0, 1)
            group(NG, over=True)

            def ut_hi(a, b, k):
                act.wait_ge(turned_u, a + k + 1)
                if past(a + k - 1):
                    act.wait_ge(w4_done, a + k - 1)
                act.activation(ut[0][:, k % 2].rearrange("p c n -> p (c n)"), ps[:, BLOCK + 2 + k % 2, :],
                               ACT.Copy).then_inc(ut_hi_ready, 1)

            def node_exp(a, b, k):
                act.wait_ge(v_ready, a + k + 1)
                act.wait_ge(mish_ready, M0 + a + k - 1)
                act.activation(e_buf[:, k % 2, :], v_row[:, k % RING, :], ACT.Exp).then_inc(e_ready, 1)

            def node_square(a, b, k):
                act.wait_ge(e_held, M0 + a + k + 1)
                act.wait_ge(mish_ready, M0 + a + k - 1)
                act.activation(n_buf[:, k % 2, :], e_buf[:, k % 2, :], ACT.Square).then_inc(n_ready, 1)

            def node_ln(a, b, k):
                act.wait_ge(n_ready, M0 + a + k + 1)
                act.activation(e_buf[:, k % 2, :], n_buf[:, k % 2, :], ACT.Ln, bias=1.0).then_inc(ln_done, 1)

            def node_inverse(a, b, k):
                act.wait_ge(ln_done, M0 + a + k + 1)
                act.activation(e_buf[:, k % 2, :], e_buf[:, k % 2, :], ACT.Exp, scale=-1.0).then_inc(inv_ready, 1)

            def squares_y(a, b, k):
                q = k % RING
                act.wait_ge(nmean1_ready, a + k + 1)
                if past(a + k):
                    act.wait_ge(squared1, a + k)
                act.activation(unused[:, 0, :], y_row[:, q, :], ACT.Square, bias=nmean1[:, q:q + 1],
                               accum_out=ssq1[:, q:q + 1]).then_inc(squared1, 1)

            def squares_w(a, b, k):
                q = k % RING
                act.wait_ge(nmean2_ready, a + k + 1)
                if past(a + k):
                    act.wait_ge(squared2, a + k)
                act.activation(unused[:, 1, :], w_row[:, k % 2, :], ACT.Square, bias=nmean2[:, q:q + 1],
                               accum_out=ssq2[:, q:q + 1]).then_inc(squared2, 1)

            def final(a, b, k):
                q = k % RING
                act.wait_ge(shift2_ready, a + k + 1)
                if past(16 * (b + k // RING)):
                    act.wait_ge(stored[q], 16 * (b + k // RING))
                act.activation(o_row[:, q, :], w_row[:, k % 2, :], ACT.Identity, bias=shift2[:, q:q + 1],
                               scale=rstd2[:, q:q + 1]).then_inc(normed, 1)

            def step(a, b, k, live):
                if live(a, k - 5):
                    final(a, b, k - 5)
                if live(a, k - 1):
                    node_exp(a, b, k - 1)
                if live(a, k + 1):
                    xt_hi(a, b, k + 1)
                if live(a, k - 1):
                    node_square(a, b, k - 1)
                    node_ln(a, b, k - 1)
                if live(a, k - 4):
                    squares_w(a, b, k - 4)
                if live(a, k - 1):
                    node_inverse(a, b, k - 1)
                if live(a, k - 3):
                    squares_y(a, b, k - 3)
                if live(a, k - 2):
                    ut_hi(a, b, k - 2)

            run_steps(act, step, 1)

        @block.vector
        def _(dve):
            def weight_lo(i, out_, in_, hi):
                dve.wait_ge(w_hi_ready, i + 1)
                dve.tensor_tensor(out_, in_, hi.bitcast(F32), ALU.subtract).then_inc(w_split, 1)

            def mish_n(slot, width, i):
                e = e_buf[:, slot, 0:width]
                dve.wait_ge(e_ready, i + 1)
                dve.tensor_scalar(e, e, E_MAX, None, ALU.min).then_inc(e_held, 1)
                dve.wait_ge(e_held, i + 1)
                if past(i - 1):
                    dve.wait_ge(mish_ready, i - 1)
                dve.scalar_tensor_tensor(out=n_buf[:, slot, 0:width], in0=e, scalar=2.0, in1=e,
                                         op0=ALU.add, op1=ALU.mult).then_inc(n_ready, 1)

            def block_vn(g, b):
                i = NB * g + b
                bias = (b1_col if b < KC else b2_col)[:, b % KC:b % KC + 1]
                dve.wait_ge(n_ready, i + 1)
                dve.wait_ge(ln_done, i + 1)
                dve.scalar_tensor_tensor(out=n_buf[:, b % 2, 0:GE], in0=ps[:, BLOCK + b % KC, 0:GE], scalar=bias,
                                         in1=n_buf[:, b % 2, 0:GE], op0=ALU.add, op1=ALU.mult).then_inc(vn_ready, 1)

            def mish_f(slot, width, i):
                dve.wait_ge(inv_ready, i + 1)
                dve.wait_ge(vn_ready, i + 1)
                dve.tensor_tensor(f_buf[:, slot, 0:width], n_buf[:, slot, 0:width], e_buf[:, slot, 0:width],
                                  ALU.mult).then_inc(mish_ready, 1)

            def block_lo(g, b):
                i = NB * g + b
                t = ht if b < KC else mt
                dve.wait_ge(mish_hi_ready, i + 1)
                dve.tensor_tensor(t[1][:, b % KC, :], f_buf[:, b % 2, 0:GE], t[0][:, b % KC, :].bitcast(F32),
                                  ALU.subtract).then_inc(mish_split, 1)

            def mish_blocks(g, first_block):
                for b in range(first_block, first_block + KC):
                    mish_n(b % 2, GE, NB * g + b)
                    if b > first_block:
                        block_lo(g, b - 1)
                    block_vn(g, b)
                    if past(NB * g + b - 1):
                        dve.wait_ge(mish_hi_ready, NB * g + b - 1)
                    if past(NB * g + b - 1):
                        dve.wait_ge(mish_split, NB * g + b - 1)
                    mish_f(b % 2, GE, NB * g + b)
                block_lo(g, first_block + KC - 1)

            def ft_lo(g, c):
                dve.wait_ge(ft_hi_ready, XC * g + c + 1)
                dve.tensor_tensor(ft[1][:, c, :], ps[:, TURN + c % 2, 0:GE], ft[0][:, c, :].bitcast(F32),
                                  ALU.subtract).then_inc(ft_split, 1)

            def ea_out(g):
                dve.wait_ge(turned_ea, g + 1)
                dve.tensor_copy(eat, ps[:, TURN, 0:GE]).then_inc(eat_ready, 1)

            def ea_split(g):
                rows = ea_all[0:LE, bass.ds(g * GT, GT), :]
                if past(g):
                    dve.wait_ge(turned_ea, g)
                dve.tensor_copy(ea_cat[0:LE, :, 0:D], rows).then_inc(ea_hi_ready, 1)
                dve.wait_ge(ea_hi_ready, g + 1)
                dve.tensor_tensor(ea_cat[0:LE, :, D:2 * D], rows, ea_cat[0:LE, :, 0:D].bitcast(F32),
                                  ALU.subtract).then_inc(ea_cat_ready, 1)

            def z_lo(g, j):
                dve.wait_ge(z_hi_ready, GT * g + j + 1)
                dve.tensor_tensor(zs[1][0:LE, j % 2, :], ps[0:LE, ROWS + j % 2, :], zs[0][0:LE, j % 2, :].bitcast(F32),
                                  ALU.subtract).then_inc(z_split, 1)

            def same_dst(g):
                dve.wait_ge(turned_dst, g + 1)
                if past(GT * g):
                    dve.wait_ge(sum_done, GT * g)
                for j in range(GT):
                    dve.tensor_scalar(same[0:LE, j, :], ps[0:LE, TURN + 1, j * LE:(j + 1) * LE],
                                      dst_sum[0:LE, j:j + 1], None, ALU.is_equal).then_inc(same_part_ready, 1)
                dve.wait_ge(same_part_ready, GT * (g + 1))
                dve.tensor_tensor(same_below[0:LE], same[0:LE].bitcast(F32),
                                  below[0:LE].rearrange("p (a n) -> p a n", a=1).to_broadcast([LE, GT, LE]),
                                  ALU.mult).then_inc(same_ready, 1)
                dve.wait_ge(same_ready, g + 1)
                dve.tensor_reduce(n_before[0:LE, :], same_below[0:LE], AX.X, ALU.add).then_inc(counted, 1)
                if past(g):
                    dve.wait_ge(add_row_ready, g)
                dve.tensor_scalar(to_unread, dst_sum, unread_f, -1.0, ALU.subtract, ALU.mult).then_inc(distance, 1)
                dve.wait_ge(counted, g + 1)
                dve.wait_ge(distance, g + 1)
                dve.scalar_tensor_tensor(out=to_unread, in0=n_before, scalar=1.0, in1=to_unread, op0=ALU.min,
                                         op1=ALU.mult).then_inc(moved, 1)
                dve.wait_ge(moved, g + 1)
                if past(16 * GT * g):
                    dve.wait_ge(added, 16 * GT * g)
                dve.tensor_tensor(add_row, to_unread, dst_sum, ALU.add).then_inc(add_row_ready, 1)

            def take_dst(g):
                if past(g):
                    dve.wait_ge(add_row_ready, g)
                dve.tensor_copy(dst_sum, dst_f[:, bass.ds(g * GT, GT)]).then_inc(dst_sum_ready, 1)

            def group(g, first=False, last=False, over=False):
                ahead = not last and not over
                if not first:
                    same_dst(g - 1)
                if not over:
                    take_dst(g)
                if ahead:
                    ea_split(g + 1)
                if not over:
                    mish_blocks(g, 0)
                if not first:
                    z_lo(g - 1, 0)
                    z_lo(g - 1, 1)
                if ahead:
                    for c in range(0, 4):
                        ft_lo(g + 1, c)
                if not first:
                    z_lo(g - 1, 2)
                if ahead:
                    for c in range(4, 6):
                        ft_lo(g + 1, c)
                if not first:
                    z_lo(g - 1, 3)
                if ahead:
                    for c in range(6, 8):
                        ft_lo(g + 1, c)
                    ea_out(g + 1)
                if last:
                    for i, w in enumerate((w3a, w4)):
                        for c in range(KC):
                            weight_lo(XC + 1 + (2 + i) * KC + c, w[1][:, c, :], w34_in[:, i * KC + c, :],
                                         w[0][:, c, :])
                if not over:
                    mish_blocks(g, KC)

            dve.wait_ge(loaded_ea, 16)
            ea_split(0)
            dve.wait_ge(loaded_pad, 16)
            dve.wait_ge(unread_set, 1)
            dve.tensor_copy(dst_f, dst_pad).then_inc(dst_float, 1)
            dve.tensor_copy(unread_f, unread_i).then_inc(dst_float, 1)
            for c in range(XC):
                weight_lo(c, w1[1][:, c, :], w1_in[:, c, :], w1[0][:, c, :])
                ft_lo(0, c)
            weight_lo(XC, w1e[1], w1e_in, w1e[0])
            ea_out(0)
            for c in range(KC):
                weight_lo(XC + 1 + c, w2[1][:, c, :], w2_in[:, c, :], w2[0][:, c, :])
            for c in range(KC):
                weight_lo(XC + 1 + KC + c, w3b[1][:, c, :], w3b_in[:, c, :], w3b[0][:, c, :])
            dve.wait_ge(loaded_bias, 32)
            dve.wait_ge(dst_float, 2)
            dve.wait_ge(constants_made, 7)
            group(0, first=True)
            group(1)
            with dve.Fori(2, NG - 1) as g:
                group(g)
            group(NG - 1, last=True)

            M0 = NB * NG

            def xt_lo(a, b, k):
                dve.wait_ge(xt_hi_ready, a + k + 1)
                dve.tensor_tensor(xt[1][:, k % 2].rearrange("p c n -> p (c n)"), ps[:, TURN + k % 2, :],
                                  xt[0][:, k % 2].rearrange("p c n -> p (c n)").bitcast(F32),
                                  ALU.subtract).then_inc(xt_split, 1)

            def ut_lo(a, b, k):
                dve.wait_ge(ut_hi_ready, a + k + 1)
                dve.tensor_tensor(ut[1][:, k % 2].rearrange("p c n -> p (c n)"), ps[:, BLOCK + 2 + k % 2, :],
                                  ut[0][:, k % 2].rearrange("p c n -> p (c n)").bitcast(F32),
                                  ALU.subtract).then_inc(ut_split, 1)

            xt_lo(0, 0, 0)
            xt_lo(0, 0, 1)
            group(NG, over=True)
            dve.wait_ge(loaded_rows, 48)
            dve.wait_ge(mish_hi_ready, M0)
            dve.wait_ge(mish_split, M0)

            def add_pre(a, b, k):
                q = k % RING
                dve.wait_ge(w3_done, a + k + 1)
                dve.wait_ge(pre_in[q], 16 * (b + k // RING + 1))
                dve.tensor_tensor(v_row[:, q, :], ps[:, BLOCK + k % 2, :], v_row[:, q, :], ALU.add).then_inc(v_ready, 1)

            def node_held(a, b, k):
                e = e_buf[:, k % 2, :]
                dve.wait_ge(e_ready, M0 + a + k + 1)
                dve.tensor_scalar(e, e, E_MAX, 1.0, ALU.min, ALU.add).then_inc(e_held, 1)

            def node_vn(a, b, k):
                q = k % RING
                dve.wait_ge(n_ready, M0 + a + k + 1)
                dve.scalar_tensor_tensor(out=v_row[:, q, :], in0=n_buf[:, k % 2, :], scalar=-1.0, in1=v_row[:, q, :],
                                         op0=ALU.add, op1=ALU.mult).then_inc(vn_ready, 1)

            def node_f(a, b, k):
                dve.wait_ge(inv_ready, M0 + a + k + 1)
                dve.wait_ge(vn_ready, M0 + a + k + 1)
                if past(a + k - 1):
                    dve.wait_ge(turned_u, a + k - 1)
                dve.tensor_tensor(f_buf[:, k % 2, :], v_row[:, k % RING, :], e_buf[:, k % 2, :],
                                  ALU.mult).then_inc(mish_ready, 1)

            def residual(a, b, k):
                q = k % RING
                dve.wait_ge(w4_done, a + k + 1)
                dve.wait_ge(x_b4, a + k + 1)
                dve.scalar_tensor_tensor(out=y_row[:, q, :], in0=ps[:, ROWS + k % 2, :], scalar=1.0, in1=y_row[:, q, :],
                                         op0=ALU.mult, op1=ALU.add,
                                         accum_out=sum1[:, q:q + 1]).then_inc(y_ready, 1)

            def norm_gamma(a, b, k):
                q = k % RING
                dve.wait_ge(nmean1_ready, a + k + 1)
                dve.wait_ge(squared1, a + k + 1)
                dve.scalar_tensor_tensor(out=y_row[:, q, :], in0=y_row[:, q, :], scalar=nmean1[:, q:q + 1],
                                         in1=gamma_row, op0=ALU.add, op1=ALU.mult).then_inc(y_gamma_ready, 1)

            def residual2(a, b, k):
                q = k % RING
                dve.wait_ge(rstd1_ready, a + k + 1)
                if past(a + k - 1):
                    dve.wait_ge(normed, a + k - 1)
                dve.wait_ge(y_gamma_ready, a + k + 1)
                dve.wait_ge(x_beta, a + k + 1)
                dve.scalar_tensor_tensor(out=w_row[:, k % 2, :], in0=y_row[:, q, :], scalar=rstd1[:, q:q + 1],
                                         in1=xb_row[:, q, :], op0=ALU.mult, op1=ALU.add,
                                         accum_out=sum2[:, q:q + 1]).then_inc(w_ready, 1)

            def step(a, b, k, live):
                if live(a, k - 1):
                    add_pre(a, b, k - 1)
                if live(a, k - 4):
                    norm_gamma(a, b, k - 4)
                if live(a, k - 1):
                    node_held(a, b, k - 1)
                if live(a, k - 4):
                    residual2(a, b, k - 4)
                if live(a, k + 1):
                    xt_lo(a, b, k + 1)
                if live(a, k - 3):
                    residual(a, b, k - 3)
                if live(a, k - 1):
                    node_vn(a, b, k - 1)
                    node_f(a, b, k - 1)
                if live(a, k - 2):
                    ut_lo(a, b, k - 2)

            run_steps(dve, step, 1)


_INS = ["x", "src", "dst", "edge_attr_64"] + [
    f"L0_gnn_{n}" for n in ("W1", "b1", "W2", "b2", "W3", "b3", "W4", "b4", "gamma", "beta")]


def kernel(**inputs):
    import numpy as np
    import concourse.bacc as bacc
    from concourse.bass_utils import run_bass_kernel_spmd

    nc = bacc.Bacc("TRN2", target_bir_lowering=False, num_devices=1)
    arrays, args = {}, []
    for name in _INS:
        a = np.ascontiguousarray(inputs[name])
        arrays[f"in_{name}"] = a
        args.append(nc.dram_tensor(f"in_{name}", a.shape, mybir.dt.from_np(a.dtype), kind="ExternalInput").ap())
    out = nc.dram_tensor("out_rows", inputs["x"].shape, F32, kind="ExternalOutput").ap()
    gnn_kernel(nc, *args, out)
    r = run_bass_kernel_spmd(nc, [arrays], core_ids=[0])
    return r.results[0]["out_rows"]
```

```python
import concourse.bass as bass
from concourse import mybir

ACT = mybir.ActivationFunctionType
ALU = mybir.AluOpType
AX = mybir.AxisListType
F32 = mybir.dt.float32
F32R = mybir.dt.float32r
I32 = mybir.dt.int32
BF16 = mybir.dt.bfloat16

P = 128
E_MAX = float(2 ** 14)
EPS = 1e-5
RING = 4


def gnn_kernel(nc, x, src, dst, edge_attr, W1, b1, W2, b2, W3, b3, W4, b4, gamma, beta, out):
    N, H = x.shape
    E, D = edge_attr.shape
    KC = H // P
    LE = 125
    ET = E // LE
    GT = 4
    NG = ET // GT
    GE = GT * LE
    XC = 2 * KC
    NB = 2 * KC
    NT = -(-N // P)
    PIECE = 4
    PIECES = -(-(NT + 1) // PIECE)
    AHEAD = 4
    WARM = 36
    LAST = N - P
    PT = NT + 1
    assert LE * ET == E and NG * GT == ET and 2 * D == P and KC == GT == RING == 4 and NG >= 4

    pre = nc.dram_tensor("pre_table", (PT * P, H), F32).ap()

    start = -(-nc.sbuf_base // 64) * 64
    end = nc.sbuf_usable_end
    at = [start]

    def place(name, shape, dt, offset=None):
        size = 2 if dt == BF16 else 4
        for n in shape[1:]:
            size *= n
        if offset is None:
            offset = at[0]
            at[0] += -(-size // 32) * 32
        assert offset + size <= end, name
        return nc.alloc_sbuf_tensor_at(name, shape, dt, offset=offset).ap()

    ident = place("ident", [P, P], F32)
    below = place("below", [P, LE], F32)
    b1_col = place("b1_col", [P, KC], F32)
    b2_col = place("b2_col", [P, KC], F32)
    b3_row = place("b3_row", [P, H], F32)
    b4_row = place("b4_row", [P, H], F32)
    gamma_row = place("gamma_row", [P, H], F32)
    beta_row = place("beta_row", [P, H], F32)
    src_all = place("src_all", [P, ET], I32)
    dst_all = place("dst_all", [P, ET], I32)
    dst_pad = place("dst_pad", [P, ET], I32)
    dst_f = place("dst_f", [P, ET], F32)
    unread_i = place("unread_i", [P, 1], I32)
    unread_f = place("unread_f", [P, 1], F32)
    src_now = place("src_now", [P, GT], I32)
    dst_now = place("dst_now", [P, GT], I32)
    dst_sum = place("dst_sum", [P, GT], F32)
    n_before = place("n_before", [P, GT], F32)
    to_unread = place("to_unread", [P, GT], F32)
    add_row = place("add_row", [P, GT], I32)
    minus_half = place("minus_half", [P, 1], F32)
    sum1, nmean1, ssq1, var1, rstd1 = (place(k + "1", [P, RING], F32) for k in ("sum", "nmean", "ssq", "var", "rstd"))
    sum2, nmean2, ssq2, var2, rstd2 = (place(k + "2", [P, RING], F32) for k in ("sum", "nmean", "ssq", "var", "rstd"))
    shift2 = place("shift2", [P, RING], F32)
    e_buf = place("e_buf", [P, 2, H], F32)
    n_buf = place("n_buf", [P, 2, H], F32)
    f_buf = place("f_buf", [P, 2, H], F32)
    w2 = [place(f"w2_{s}", [P, KC, H], F32R) for s in ("hi", "lo")]
    w3b = [place(f"w3b_{s}", [P, KC, H], F32R) for s in ("hi", "lo")]
    at_w1 = at[0]
    w1 = [place(f"w1_{s}", [P, XC, H], F32R) for s in ("hi", "lo")]
    w1e = [place(f"w1e_{s}", [P, H], F32R) for s in ("hi", "lo")]
    at_ft = at[0]
    ft = [place(f"ft_{s}", [P, XC, GE], F32R) for s in ("hi", "lo")]
    eat = place("eat", [P, GE], F32R)
    at_xg = at[0]
    xg = place("xg", [P, 2 * GT, H], F32)
    at_h = at[0]
    ht = [place(f"ht_{s}", [P, KC, GE], F32R) for s in ("hi", "lo")]
    mt = [place(f"mt_{s}", [P, KC, GE], F32R) for s in ("hi", "lo")]
    same = place("same", [P, GT, LE], F32R)
    same_below = place("same_below", [P, GT, LE], F32)
    at_ea = at[0]
    ea_cat = place("ea_cat", [P, GT, P], F32R)
    at_z = at[0]
    zs = [place(f"z_{s}", [P, 2, H], F32R) for s in ("hi", "lo")]
    agg = place("agg", [P, GT, H], F32)
    ea_all = place("ea_all", [P, ET, D], F32)
    at_end = at[0]

    w1_in = place("w1_in", [P, XC, H], F32, at_h)
    w2_in = place("w2_in", [P, KC, H], F32, at_h + XC * H * 4)
    w3b_in = place("w3b_in", [P, KC, H], F32, at_h + (XC + KC) * H * 4)
    w1e_in = place("w1e_in", [P, H], F32, at_z)
    assert at_h + (XC + 2 * KC) * H * 4 <= at_ea

    w3a = [place(f"w3a_{s}", [P, KC, H], F32R, at_w1 + i * KC * H * 4) for i, s in enumerate(("hi", "lo"))]
    w4 = [place(f"w4_{s}", [P, KC, H], F32R, at_w1 + (2 + i) * KC * H * 4) for i, s in enumerate(("hi", "lo"))]
    w34_in = place("w34_in", [P, 2 * KC, H], F32, at_xg)
    at[0] = at_ft
    xt = [place(f"xt_{s}", [P, 2, KC, P], F32R) for s in ("hi", "lo")]
    ut = [place(f"ut_{s}", [P, 2, KC, P], F32R) for s in ("hi", "lo")]
    x_row = place("x_row", [P, RING, H], F32)
    y_row = place("y_row", [P, RING, H], F32)
    assert at[0] <= at_xg
    at[0] = at_h
    xb_row = place("xb_row", [P, RING, H], F32)
    w_row = place("w_row", [P, 2, H], F32)
    v_row = place("v_row", [P, RING, H], F32)
    o_row = place("o_row", [P, RING, H], F32)
    unused = place("unused", [P, 2, H], BF16)
    assert at[0] <= at_end

    ps = nc.alloc_psum_tensor("ps", [P, 8, H], F32).ap()
    BLOCK, TURN, ROWS = 0, 4, 6

    pads_set = nc.alloc_semaphore("pads_set")
    loaded_src = nc.alloc_semaphore("loaded_src")
    loaded_dst = nc.alloc_semaphore("loaded_dst")
    loaded_pad = nc.alloc_semaphore("loaded_pad")
    loaded_ea_first = nc.alloc_semaphore("loaded_ea_first")
    loaded_ea_rest = nc.alloc_semaphore("loaded_ea_rest")
    loaded_w1a = nc.alloc_semaphore("loaded_w1a")
    loaded_w1b = nc.alloc_semaphore("loaded_w1b")
    loaded_w1e = nc.alloc_semaphore("loaded_w1e")
    loaded_w2 = nc.alloc_semaphore("loaded_w2")
    loaded_w3b = nc.alloc_semaphore("loaded_w3b")
    loaded_w3a = nc.alloc_semaphore("loaded_w3a")
    loaded_w4 = nc.alloc_semaphore("loaded_w4")
    loaded_bias = nc.alloc_semaphore("loaded_bias")
    loaded_b3 = nc.alloc_semaphore("loaded_b3")
    loaded_rows = nc.alloc_semaphore("loaded_rows")
    ident_made = nc.alloc_semaphore("ident_made")
    constants_made = nc.alloc_semaphore("constants_made")
    unread_set = nc.alloc_semaphore("unread_set")
    dst_float = nc.alloc_semaphore("dst_float")
    w_hi_ready = nc.alloc_semaphore("w_hi_ready")
    w_split = nc.alloc_semaphore("w_split")
    table_set = [nc.alloc_semaphore(f"table_set{i}") for i in range(2)]
    added = nc.alloc_semaphore("added")
    src_staged = nc.alloc_semaphore("src_staged")
    dst_staged = nc.alloc_semaphore("dst_staged")
    turned_x = nc.alloc_semaphore("turned_x")
    ft_hi_ready = nc.alloc_semaphore("ft_hi_ready")
    ft_split = nc.alloc_semaphore("ft_split")
    ea_hi_ready = nc.alloc_semaphore("ea_hi_ready")
    ea_cat_ready = nc.alloc_semaphore("ea_cat_ready")
    turned_ea = nc.alloc_semaphore("turned_ea")
    eat_ready = nc.alloc_semaphore("eat_ready")
    block_done = nc.alloc_semaphore("block_done")
    e_ready = nc.alloc_semaphore("e_ready")
    e_held = nc.alloc_semaphore("e_held")
    n_ready = nc.alloc_semaphore("n_ready")
    ln_done = nc.alloc_semaphore("ln_done")
    inv_ready = nc.alloc_semaphore("inv_ready")
    vn_ready = nc.alloc_semaphore("vn_ready")
    mish_ready = nc.alloc_semaphore("mish_ready")
    mish_hi_ready = nc.alloc_semaphore("mish_hi_ready")
    mish_split = nc.alloc_semaphore("mish_split")
    z_done = nc.alloc_semaphore("z_done")
    z_hi_ready = nc.alloc_semaphore("z_hi_ready")
    z_split = nc.alloc_semaphore("z_split")
    sum_done = nc.alloc_semaphore("sum_done")
    agg_ready = nc.alloc_semaphore("agg_ready")
    dst_sum_ready = nc.alloc_semaphore("dst_sum_ready")
    turned_dst = nc.alloc_semaphore("turned_dst")
    same_part_ready = nc.alloc_semaphore("same_part_ready")
    same_ready = nc.alloc_semaphore("same_ready")
    counted = nc.alloc_semaphore("counted")
    distance = nc.alloc_semaphore("distance")
    moved = nc.alloc_semaphore("moved")
    add_row_ready = nc.alloc_semaphore("add_row_ready")
    turned_node = nc.alloc_semaphore("turned_node")
    xt_hi_ready = nc.alloc_semaphore("xt_hi_ready")
    xt_split = nc.alloc_semaphore("xt_split")
    w3_done = nc.alloc_semaphore("w3_done")
    v_ready = nc.alloc_semaphore("v_ready")
    turned_u = nc.alloc_semaphore("turned_u")
    ut_hi_ready = nc.alloc_semaphore("ut_hi_ready")
    ut_split = nc.alloc_semaphore("ut_split")
    w4_done = nc.alloc_semaphore("w4_done")
    x_b4 = nc.alloc_semaphore("x_b4")
    x_beta = nc.alloc_semaphore("x_beta")
    y_ready = nc.alloc_semaphore("y_ready")
    nmean1_ready = nc.alloc_semaphore("nmean1_ready")
    squared1 = nc.alloc_semaphore("squared1")
    var1_ready = nc.alloc_semaphore("var1_ready")
    rstd1_ready = nc.alloc_semaphore("rstd1_ready")
    y_gamma_ready = nc.alloc_semaphore("y_gamma_ready")
    w_ready = nc.alloc_semaphore("w_ready")
    nmean2_ready = nc.alloc_semaphore("nmean2_ready")
    squared2 = nc.alloc_semaphore("squared2")
    var2_ready = nc.alloc_semaphore("var2_ready")
    rstd2_ready = nc.alloc_semaphore("rstd2_ready")
    shift2_ready = nc.alloc_semaphore("shift2_ready")
    normed = nc.alloc_semaphore("normed")
    src_in = [nc.alloc_semaphore(f"src_in{j}") for j in range(GT)]
    dst_in = [nc.alloc_semaphore(f"dst_in{j}") for j in range(GT)]
    x_in = [nc.alloc_semaphore(f"x_in{j}") for j in range(RING)]
    pre_in = [nc.alloc_semaphore(f"pre_in{j}") for j in range(RING)]
    stored = [nc.alloc_semaphore(f"stored{j}") for j in range(RING)]

    def past(count):
        return not isinstance(count, int) or count > 0

    def split_matmul(pe, out_, lhs, rhs, first, last):
        pe.matmul(out_, lhs[0], rhs[0], start=first, stop=False)
        pe.matmul(out_, lhs[0], rhs[1], start=False, stop=False)
        return pe.matmul(out_, lhs[1], rhs[0], start=False, stop=last)

    def ahead(a, k):
        return isinstance(a, int) and a + k < AHEAD

    def w3_bank(a, k):
        return BLOCK + (k if ahead(a, k) else k % 2)

    def run_steps(eng, step, begin):
        first, end = 3, (NT - 2 - 3 - (RING - 1)) // RING + 1
        inside = lambda a, k: 0 <= a + k < NT
        for k in range(begin, RING * first):
            step(0, 0, k, inside)
        with eng.Fori(first, end) as b:
            for k in range(RING):
                step(RING * b, b, k, lambda a, k: True)
        for k in range(RING * end, NT + 6):
            step(0, 0, k, inside)

    with nc.Block() as block:

        @block.sync
        def _(sp):
            def row(v):
                return v.rearrange("(a d) -> a d", a=1).to_broadcast([P, H])

            sp.wait_ge(pads_set, 3)
            sp.dma_start(src_all[0:LE, :], src.rearrange("(p t) -> p t", t=ET)).then_inc(loaded_src, 16)
            sp.dma_start(dst_all[0:LE, :], dst.rearrange("(p t) -> p t", t=ET)).then_inc(loaded_dst, 16)
            ea_rows = edge_attr.rearrange("(p t) d -> p t d", t=ET)
            w1_rows = W1[0:2 * H, :].rearrange("(c p) n -> p c n", p=P)
            sp.dma_start(w1_in[:, 0:KC, :], w1_rows[:, 0:KC, :]).then_inc(loaded_w1a, 16)
            sp.dma_start(ea_all[0:LE, 0:GT], ea_rows[:, 0:GT]).then_inc(loaded_ea_first, 16)
            sp.wait_ge(src_in[0], 16)
            sp.dma_start(w1_in[:, KC:XC, :], w1_rows[:, KC:XC, :]).then_inc(loaded_w1b, 16)
            for i in range(2):
                sp.dma_start(w1e_in[i * D:(i + 1) * D, :], W1[2 * H:2 * H + D, :]).then_inc(loaded_w1e, 16)
            sp.dma_start(b1_col, b1.rearrange("(c p) -> p c", p=P),
                         allow_slow_non_contiguous=True).then_inc(loaded_bias, 16)
            sp.dma_start(b2_col, b2.rearrange("(c p) -> p c", p=P),
                         allow_slow_non_contiguous=True).then_inc(loaded_bias, 16)
            sp.dma_start(dst_pad[0:LE, :], dst.rearrange("(p t) -> p t", t=ET)).then_inc(loaded_pad, 16)
            for j in range(GT):
                sp.wait_ge(dst_in[j], 16)
            sp.dma_start(w2_in, W2.rearrange("(c p) n -> p c n", p=P)).then_inc(loaded_w2, 16)
            sp.dma_start(ea_all[0:LE, GT:ET], ea_rows[:, GT:ET]).then_inc(loaded_ea_rest, 16)
            sp.dma_start(w3b_in, W3[H:2 * H, :].rearrange("(c p) n -> p c n", p=P)).then_inc(loaded_w3b, 16)
            sp.dma_start(b3_row, row(b3)).then_inc(loaded_b3, 16)
            sp.wait_ge(loaded_b3, 16)
            for i in range(PIECES):
                t, n = i * PIECE, min(PIECE, PT - i * PIECE)
                if i >= 2:
                    sp.wait_ge(table_set[i % 2], 16 * (i // 2))
                sp.dma_start(pre[t * P:(t + n) * P, :].rearrange("(n p) d -> p n d", p=P),
                             b3_row.rearrange("p (a d) -> p a d", a=1).to_broadcast([P, n, H])
                             ).then_inc(table_set[i % 2], 16)
            for tile_, v in ((b4_row, b4), (gamma_row, gamma), (beta_row, beta)):
                sp.dma_start(tile_, row(v)).then_inc(loaded_rows, 16)

            sp.wait_ge(turned_x, XC * NG)
            sp.dma_start(w34_in[:, 0:KC, :], W3[0:H, :].rearrange("(c p) n -> p c n", p=P)).then_inc(loaded_w3a, 16)
            sp.dma_start(w34_in[:, KC:2 * KC, :], W4.rearrange("(c p) n -> p c n", p=P)).then_inc(loaded_w4, 16)
            sp.wait_ge(block_done, NB * (NG - 1) + KC)

            def rows_of(a, b, k):
                t = a + k
                return slice(LAST, LAST + P) if isinstance(t, int) and t == NT - 1 else bass.ds(t * P, P)

            def load_x(a, b, k):
                if past(a + k - RING + 1):
                    sp.wait_ge(turned_node, a + k - RING + 1)
                if past(a + k - RING + 1):
                    sp.wait_ge(x_beta, a + k - RING + 1)
                sp.dma_start(x_row[:, k % RING, :], x[rows_of(a, b, k), :]).then_inc(x_in[k % RING], 16)

            def load_pre(a, b, k):
                sp.wait_ge(mish_ready, NB * NG + a + k - RING + 1)
                sp.dma_start(v_row[:, k % RING, :], pre[rows_of(a, b, k), :]).then_inc(pre_in[k % RING], 16)

            def store(a, b, k):
                sp.wait_ge(normed, a + k + 1)
                t = a + k
                if isinstance(t, int) and t == NT - 1:
                    skip = NT * P - N
                    sp.dma_start(out[LAST + skip:N, :], o_row[skip:P, k % RING, :]).then_inc(stored[k % RING], 16)
                else:
                    sp.dma_start(out[bass.ds(t * P, P), :], o_row[:, k % RING, :]).then_inc(stored[k % RING], 16)

            def step(a, b, k, live):
                if live(a, k + 3) and not ahead(a, k + 3):
                    load_x(a, b, k + 3)
                if live(a, k + 2) and not ahead(a, k + 2):
                    load_pre(a, b, k + 2)
                if live(a, k - 6):
                    store(a, b, k - 6)

            for k in range(AHEAD):
                load_x(0, 0, k)
            sp.wait_ge(added, 16 * ET)
            for k in range(AHEAD):
                load_pre(0, 0, k)
            run_steps(sp, step, 0)
            for j in range(RING):
                sp.wait_ge(stored[j], 16 * len(range(j, NT, RING)))

        @block.gpsimd
        def _(pool):
            pool.memset(src_all, 0).then_inc(pads_set, 1)
            pool.memset(dst_all, 0).then_inc(pads_set, 1)
            pool.iota(unread_i, [[0, 1]], base=NT * P, channel_multiplier=1).then_inc(unread_set, 1)
            pool.iota(dst_pad, [[0, ET]], base=NT * P, channel_multiplier=1).then_inc(pads_set, 1)

            def to_count(count):
                return count if isinstance(count, int) else pool.to_reg(count)


            def gather_src(g):
                if past(XC * (g - 1) + KC):
                    pool.wait_ge(turned_x, XC * (g - 1) + KC)
                pool.tensor_copy(src_now, src_all[:, bass.ds(g * GT, GT)]).then_inc(src_staged, 1)
                staged = to_count(g + 1)
                pool.wait_ge(pads_set, 3)
                pool.wait_ge(src_staged, staged)
                for j in range(GT):
                    pool.indirect_dma_start(
                        out=xg[:, j, :], out_offset=None, in_=x,
                        in_offset=bass.IndirectOffsetOnAxis(ap=src_now[:, j:j + 1], axis=0),
                    ).then_inc(src_in[j], 16)

            def gather_dst(g):
                if past(XC * g):
                    pool.wait_ge(turned_x, XC * g)
                pool.tensor_copy(dst_now, dst_all[:, bass.ds(g * GT, GT)]).then_inc(dst_staged, 1)
                staged = to_count(g + 1)
                pool.wait_ge(pads_set, 3)
                pool.wait_ge(dst_staged, staged)
                for j in range(GT):
                    pool.indirect_dma_start(
                        out=xg[:, GT + j, :], out_offset=None, in_=x,
                        in_offset=bass.IndirectOffsetOnAxis(ap=dst_now[:, j:j + 1], axis=0),
                    ).then_inc(dst_in[j], 16)

            def add_rows(g, j):
                chosen, summed, before = to_count(g + 1), to_count(GT * g + j + 1), to_count(16 * (GT * g + j))
                pool.wait_ge(pads_set, 3)
                pool.wait_ge(add_row_ready, chosen)
                pool.wait_ge(agg_ready, summed)
                if past(before):
                    pool.wait_ge(added, before)
                pool.indirect_dma_start(
                    out=pre, out_offset=bass.IndirectOffsetOnAxis(ap=add_row[:, j:j + 1], axis=0),
                    in_=agg[:, j, :], in_offset=None, compute_op=ALU.add,
                ).then_inc(added, 16)

            def group(g, last=False):
                add_rows(g - 1, 0)
                if not last:
                    gather_src(g + 2)
                add_rows(g - 1, 1)
                add_rows(g - 1, 2)
                if not last:
                    gather_dst(g + 2)
                add_rows(g - 1, 3)

            pool.memset(ident, 0.0).then_inc(ident_made, 1)
            pool.wait_ge(ident_made, 1)
            pool.affine_select(out=ident, in_=ident, compare_op=ALU.not_equal, fill=1.0, base=0,
                               pattern=[[-1, P]], channel_multiplier=1).then_inc(ident_made, 1)
            pool.wait_ge(pads_set, 3)
            pool.wait_ge(loaded_src, 16)
            gather_src(0)
            pool.wait_ge(loaded_dst, 16)
            gather_dst(0)
            gather_src(1)
            pool.memset(below, 1.0).then_inc(constants_made, 1)
            pool.memset(minus_half, -0.5).then_inc(constants_made, 1)
            pool.memset(n_before, 0.0).then_inc(constants_made, 1)
            pool.memset(agg, 0.0).then_inc(constants_made, 1)
            pool.wait_ge(constants_made, 4)
            pool.affine_select(out=below, in_=below, compare_op=ALU.is_gt, fill=0.0, base=0,
                               pattern=[[-1, LE]], channel_multiplier=1).then_inc(constants_made, 1)
            gather_dst(1)
            for g in (2, 3):
                gather_src(g)
                gather_dst(g)
            for i in range(2):
                pool.wait_ge(table_set[i], 16 * len(range(i, PIECES, 2)))
            for j in range(GT):
                add_rows(0, j)
            with pool.Fori(2, NG - 2) as g:
                group(g)
            group(NG - 2, last=True)
            group(NG - 1, last=True)
            group(NG, last=True)

            pool.wait_ge(loaded_rows, 48)

            def step(a, b, k, live):
                t1, t2 = k - 3, k - 4
                q, q1, q2 = (slice(t % RING, t % RING + 1) for t in (k, t1, t2))
                if live(a, t2):
                    count = to_count(a + t2 + 1)
                    pool.wait_ge(pads_set, 3)
                    pool.wait_ge(w_ready, count)
                    pool.tensor_scalar(nmean2[:, q2], sum2[:, q2], -1.0 / H, 0.0, ALU.mult, ALU.add).then_inc(nmean2_ready, 1)
                if live(a, k):
                    pool.wait_ge(x_in[k % RING], 16 * (b + k // RING + 1))
                    if past(a + k - RING + 1):
                        pool.wait_ge(w_ready, a + k - RING + 1)
                    pool.tensor_tensor(y_row[:, k % RING, :], x_row[:, k % RING, :], b4_row, ALU.add).then_inc(x_b4, 1)
                if live(a, t1):
                    count = to_count(a + t1 + 1)
                    pool.wait_ge(pads_set, 3)
                    pool.wait_ge(y_ready, count)
                    pool.tensor_scalar(nmean1[:, q1], sum1[:, q1], -1.0 / H, 0.0, ALU.mult, ALU.add).then_inc(nmean1_ready, 1)
                if live(a, t2):
                    count = to_count(a + t2 + 1)
                    pool.wait_ge(pads_set, 3)
                    pool.wait_ge(squared2, count)
                    pool.tensor_scalar(var2[:, q2], ssq2[:, q2], 1.0 / H, EPS, ALU.mult, ALU.add).then_inc(var2_ready, 1)
                    pool.wait_ge(var2_ready, a + t2 + 1)
                    pool.tensor_tensor(rstd2[:, q2], var2[:, q2], minus_half, ALU.pow).then_inc(rstd2_ready, 1)
                    pool.wait_ge(nmean2_ready, a + t2 + 1)
                    pool.wait_ge(rstd2_ready, a + t2 + 1)
                    pool.tensor_tensor(shift2[:, q2], rstd2[:, q2], nmean2[:, q2], ALU.mult).then_inc(shift2_ready, 1)
                if live(a, t1):
                    count = to_count(a + t1 + 1)
                    pool.wait_ge(pads_set, 3)
                    pool.wait_ge(squared1, count)
                    pool.tensor_scalar(var1[:, q1], ssq1[:, q1], 1.0 / H, EPS, ALU.mult, ALU.add).then_inc(var1_ready, 1)
                    pool.wait_ge(var1_ready, a + t1 + 1)
                    pool.tensor_tensor(rstd1[:, q1], var1[:, q1], minus_half, ALU.pow).then_inc(rstd1_ready, 1)
                if live(a, k):
                    pool.tensor_tensor(xb_row[:, k % RING, :], x_row[:, k % RING, :], beta_row,
                                       ALU.add).then_inc(x_beta, 1)

            run_steps(pool, step, 0)

        @block.tensor
        def _(pe):
            def turn_chunk(g, c):
                first, gathered = (0, src_in) if c < KC else (GT, dst_in)
                cc = c % KC
                if c == 0:
                    if past(NB * (g - 1) + KC):
                        pe.wait_ge(block_done, NB * (g - 1) + KC)
                if c == 0:
                    if past(g):
                        pe.wait_ge(eat_ready, g)
                elif c == 1:
                    if past(g - 1):
                        pe.wait_ge(same_ready, g - 1)
                    if past(XC * g):
                        pe.wait_ge(ft_split, XC * g)
                else:
                    if past(XC * g + c - 1):
                        pe.wait_ge(ft_split, XC * g + c - 1)
                for j in range(GT):
                    if cc == 0:
                        pe.wait_ge(gathered[j], 16 * (g + 1))
                    t = pe.transpose(ps[:, TURN + c % 2, j * LE:(j + 1) * LE],
                                     xg[0:LE, first + j, cc * P:(cc + 1) * P], ident[0:LE, 0:LE])
                t.then_inc(turned_x, 1)

            def turn_ea(g):
                pe.wait_ge(ea_cat_ready, g + 1)
                if past(XC * g + XC - 1):
                    pe.wait_ge(ft_split, XC * g + XC - 1)
                for j in range(GT):
                    t = pe.transpose(ps[:, TURN, j * LE:(j + 1) * LE], ea_cat[0:LE, j, :].bitcast(F32),
                                     ident[0:LE, 0:LE])
                t.then_inc(turned_ea, 1)

            def turn_dst(g):
                pe.wait_ge(dst_sum_ready, g + 1)
                if isinstance(g, int) and g == NG - 1:
                    pe.wait_ge(xt_split, 2)
                else:
                    pe.wait_ge(ft_split, XC * (g + 2))
                for j in range(GT):
                    t = pe.transpose(ps[0:LE, TURN + 1, j * LE:(j + 1) * LE],
                                     dst_sum[0:LE, j:j + 1].to_broadcast([LE, LE]), ident[0:LE, 0:LE])
                t.then_inc(turned_dst, 1)

            def w1_part(mb, c):
                split_matmul(pe, ps[:, BLOCK + mb, 0:GE], [w[:, c, mb * P:(mb + 1) * P] for w in w1],
                             [f[:, c, :] for f in ft], c == 0, False)

            def w1e_part(mb):
                cols = slice(mb * P, (mb + 1) * P)
                o = ps[:, BLOCK + mb, 0:GE]
                pe.matmul(o, w1e[0][:, cols], eat, start=False, stop=False)
                pe.matmul(o, w1e[1][0:D, cols], eat[0:D, :], start=False, stop=True).then_inc(block_done, 1)

            def w1_product(g):
                for mb in range(KC):
                    if past(NB * g + mb - KC + 1):
                        pe.wait_ge(vn_ready, NB * g + mb - KC + 1)
                    for c in range(XC):
                        if mb == 0:
                            pe.wait_ge(ft_split, XC * g + c + 1)
                        w1_part(mb, c)
                    if mb == 0:
                        pe.wait_ge(eat_ready, g + 1)
                    w1e_part(mb)

            def w2_block(g, mb):
                cols = slice(mb * P, (mb + 1) * P)
                pe.wait_ge(vn_ready, NB * g + mb + 1)
                for c in range(KC):
                    if mb == 0:
                        if isinstance(g, int) and g == 0:
                            pe.wait_ge(w_split, XC + 1 + c + 1)
                        pe.wait_ge(mish_split, NB * g + c + 1)
                    mm = split_matmul(pe, ps[:, BLOCK + mb, 0:GE], [w[:, c, cols] for w in w2],
                                      [h[:, c, :] for h in ht], c == 0, c == KC - 1)
                mm.then_inc(block_done, 1)

            def z_tile(g, j):
                if isinstance(g, int) and g == 0 and j == 0:
                    pe.wait_ge(w_split, XC + 1 + 2 * KC)
                pe.wait_ge(mish_split, NB * (g + 1))
                if past(GT * g + j - 1):
                    pe.wait_ge(agg_ready, GT * g + j - 1)
                lanes = slice(j * LE, (j + 1) * LE)
                for c in range(KC):
                    mm = split_matmul(pe, ps[0:LE, ROWS + j % 2, :], [m[:, c, lanes] for m in mt],
                                      [w[:, c, :] for w in w3b], c == 0, c == KC - 1)
                mm.then_inc(z_done, 1)

            def sum_tile(g, j):
                pe.wait_ge(same_ready, g + 1)
                pe.wait_ge(z_split, GT * g + j + 1)
                o = ps[0:LE, ROWS + j % 2, :]
                pe.matmul(o, same[0:LE, j, :], zs[0][0:LE, j % 2, :], start=True, stop=False)
                pe.matmul(o, same[0:LE, j, :], zs[1][0:LE, j % 2, :], start=False, stop=True).then_inc(sum_done, 1)

            def first_group():
                pe.wait_ge(ident_made, 2)
                for _ in range(WARM):
                    pe.transpose(ps[:, ROWS, 0:P], ident, ident)
                for c in range(0, XC, 2):
                    turn_chunk(0, c)
                    turn_chunk(0, c + 1)
                    pe.wait_ge(w_split, c // 2 + 1)
                    pe.wait_ge(ft_split, c // 2 + 1)
                    for mb in range(KC):
                        w1_part(mb, c // 2)
                turn_ea(0)
                for mb in range(KC):
                    for c in range(KC, XC):
                        if mb == 0:
                            pe.wait_ge(w_split, c + 1)
                            pe.wait_ge(ft_split, c + 1)
                        w1_part(mb, c)
                    if mb == 0:
                        pe.wait_ge(w_split, XC + 1)
                        pe.wait_ge(eat_ready, 1)
                    w1e_part(mb)
                turn_chunk(1, 0)
                turn_chunk(1, 1)
                for mb in range(KC):
                    if mb < KC - 1:
                        turn_chunk(1, 2 * mb + 2)
                        turn_chunk(1, 2 * mb + 3)
                    else:
                        turn_ea(1)
                    w2_block(0, mb)

            def group(g):
                turn_dst(g - 1)
                w1_product(g)
                z_tile(g - 1, 0)
                turn_chunk(g + 1, 0)
                turn_chunk(g + 1, 1)
                z_tile(g - 1, 1)
                sum_tile(g - 1, 0)
                turn_chunk(g + 1, 2)
                turn_chunk(g + 1, 3)
                z_tile(g - 1, 2)
                sum_tile(g - 1, 1)
                turn_chunk(g + 1, 4)
                turn_chunk(g + 1, 5)
                z_tile(g - 1, 3)
                sum_tile(g - 1, 2)
                turn_chunk(g + 1, 6)
                turn_chunk(g + 1, 7)
                w2_block(g, 0)
                sum_tile(g - 1, 3)
                turn_ea(g + 1)
                for mb in range(1, KC):
                    w2_block(g, mb)

            def last_group():
                g = NG - 1
                turn_dst(g - 1)
                w1_product(g)
                pe.wait_ge(eat_ready, NG)
                z_tile(g - 1, 0)
                z_tile(g - 1, 1)
                turn_x(0, 0, 0)
                turn_x(0, 0, 1)
                w2_block(g, 0)
                sum_tile(g - 1, 0)
                sum_tile(g - 1, 1)
                w2_block(g, 1)
                z_tile(g - 1, 2)
                z_tile(g - 1, 3)
                w2_block(g, 2)
                sum_tile(g - 1, 2)
                sum_tile(g - 1, 3)
                w2_block(g, 3)

            def last_rows():
                g = NG - 1
                turn_dst(g)
                w3_product(0, 0, 0)
                w3_product(0, 0, 1)
                z_tile(g, 0)
                z_tile(g, 1)
                sum_tile(g, 0)
                turn_x(0, 0, 2)
                z_tile(g, 2)
                sum_tile(g, 1)
                turn_x(0, 0, 3)
                z_tile(g, 3)
                sum_tile(g, 2)
                w3_product(0, 0, 2)
                sum_tile(g, 3)
                w3_product(0, 0, 3)

            def turn_x(a, b, k):
                pe.wait_ge(x_in[k % RING], 16 * (b + k // RING + 1))
                if past(a + k - 1):
                    pe.wait_ge(xt_split, a + k - 1)
                if isinstance(a, int) and a + k in (1, 3):
                    pe.wait_ge(same_ready, NG - 1 if a + k == 1 else NG)
                for c in range(KC):
                    t = pe.transpose(ps[:, TURN + k % 2, c * P:(c + 1) * P],
                                     x_row[:, k % RING, c * P:(c + 1) * P], ident)
                t.then_inc(turned_node, 1)

            def turn_u(a, b, k):
                pe.wait_ge(mish_ready, NB * NG + a + k + 1)
                if isinstance(a, int) and a + k < 2:
                    pe.wait_ge(v_ready, a + k + 3)
                else:
                    pe.wait_ge(ut_split, a + k - 1)
                for c in range(KC):
                    t = pe.transpose(ps[:, BLOCK + 2 + k % 2, c * P:(c + 1) * P],
                                     f_buf[:, k % 2, c * P:(c + 1) * P], ident)
                t.then_inc(turned_u, 1)

            def w3_product(a, b, k):
                if isinstance(a, int) and a + k == 0:
                    pe.wait_ge(w_split, XC + 1 + 3 * KC)
                pe.wait_ge(xt_split, a + k + 1)
                if ahead(a, k):
                    pe.wait_ge(vn_ready, NB * NG - KC + k + 1)
                else:
                    pe.wait_ge(v_ready, a + k - 1)
                for c in range(KC):
                    mm = split_matmul(pe, ps[:, w3_bank(a, k), :], [v[:, k % 2, c, :] for v in xt],
                                      [w[:, c, :] for w in w3a], c == 0, c == KC - 1)
                mm.then_inc(w3_done, 1)

            def w4_product(a, b, k):
                if isinstance(a, int) and a + k == 0:
                    pe.wait_ge(w_split, XC + 1 + 4 * KC)
                pe.wait_ge(ut_split, a + k + 1)
                if past(a + k - 1):
                    pe.wait_ge(y_ready, a + k - 1)
                for c in range(KC):
                    mm = split_matmul(pe, ps[:, ROWS + k % 2, :], [v[:, k % 2, c, :] for v in ut],
                                      [w[:, c, :] for w in w4], c == 0, c == KC - 1)
                mm.then_inc(w4_done, 1)

            def step(a, b, k, live):
                if live(a, k + 1) and not ahead(a, k + 1):
                    turn_x(a, b, k + 1)
                if live(a, k - 3):
                    w4_product(a, b, k - 3)
                if live(a, k - 2):
                    turn_u(a, b, k - 2)
                if live(a, k) and not ahead(a, k):
                    w3_product(a, b, k)

            first_group()
            group(1)
            with pe.Fori(2, NG - 1) as g:
                group(g)
            last_group()
            last_rows()
            pe.wait_ge(agg_ready, GT * NG)
            run_steps(pe, step, 2)

        @block.scalar
        def _(act):
            def weight_hi(out_, in_):
                act.activation(out_, in_, ACT.Copy).then_inc(w_hi_ready, 1)

            def mish_exp(g, b):
                i = NB * g + b
                act.wait_ge(block_done, i + 1)
                if past(i - 1):
                    act.wait_ge(mish_ready, i - 1)
                act.activation(e_buf[:, b % 2, 0:GE], ps[:, BLOCK + b % KC, 0:GE], ACT.Exp,
                               bias=(b1_col if b < KC else b2_col)[:, b % KC:b % KC + 1]).then_inc(e_ready, 1)

            def mish_inverse(slot, width, i):
                act.wait_ge(n_ready, i + 1)
                act.activation(e_buf[:, slot, 0:width], n_buf[:, slot, 0:width], ACT.Ln, bias=2.0).then_inc(ln_done, 1)
                act.wait_ge(ln_done, i + 1)
                act.activation(e_buf[:, slot, 0:width], e_buf[:, slot, 0:width], ACT.Exp, scale=-1.0).then_inc(inv_ready, 1)

            def mish_hi(g, b):
                i = NB * g + b
                act.wait_ge(mish_ready, i + 1)
                if b < KC:
                    if past(NB * g):
                        act.wait_ge(block_done, NB * g)
                else:
                    if past(GT * g):
                        act.wait_ge(z_done, GT * g)
                act.activation((ht if b < KC else mt)[0][:, b % KC, :], f_buf[:, b % 2, 0:GE], ACT.Copy).then_inc(mish_hi_ready, 1)

            def mish_blocks(g, first_block, before_last=None, after_exp=None):
                n = KC
                mish_exp(g, first_block)
                if after_exp:
                    after_exp(first_block)
                for b in range(first_block, first_block + n):
                    mish_inverse(b % 2, GE, NB * g + b)
                    if b + 1 < first_block + n:
                        mish_exp(g, b + 1)
                        if after_exp:
                            after_exp(b + 1)
                    elif before_last:
                        before_last()
                    mish_hi(g, b)

            def ft_hi(g, c):
                act.wait_ge(turned_x, XC * g + c + 1)
                if c == 0:
                    if past(NB * (g - 1) + KC):
                        act.wait_ge(block_done, NB * (g - 1) + KC)
                act.activation(ft[0][:, c, :], ps[:, TURN + c % 2, 0:GE], ACT.Copy).then_inc(ft_hi_ready, 1)

            def z_hi(g, j):
                act.wait_ge(z_done, GT * g + j + 1)
                if past(GT * g + j - 1):
                    act.wait_ge(sum_done, GT * g + j - 1)
                act.activation(zs[0][0:LE, j % 2, :], ps[0:LE, ROWS + j % 2, :], ACT.Copy).then_inc(z_hi_ready, 1)

            def agg_out(g, j):
                act.wait_ge(sum_done, GT * g + j + 1)
                if past(16 * (GT * (g - 1) + j + 1)):
                    act.wait_ge(added, 16 * (GT * (g - 1) + j + 1))
                act.activation(agg[0:LE, j, :], ps[0:LE, ROWS + j % 2, :], ACT.Copy).then_inc(agg_ready, 1)

            def first_group():
                def more(b):
                    for c in (2 * (b - KC) + 4, 2 * (b - KC) + 5):
                        if c < XC:
                            ft_hi(1, c)

                mish_blocks(0, 0, before_last=lambda: ft_hi(1, 0))
                for c in range(1, 4):
                    ft_hi(1, c)
                mish_blocks(0, KC, after_exp=more)

            def group(g):
                def before_last():
                    z_hi(g - 1, 0)
                    ft_hi(g + 1, 0)

                mish_blocks(g, 0, before_last=before_last)
                ft_hi(g + 1, 1)
                z_hi(g - 1, 1)
                agg_out(g - 1, 0)
                ft_hi(g + 1, 2)
                ft_hi(g + 1, 3)
                z_hi(g - 1, 2)
                agg_out(g - 1, 1)
                ft_hi(g + 1, 4)
                ft_hi(g + 1, 5)
                z_hi(g - 1, 3)
                agg_out(g - 1, 2)
                ft_hi(g + 1, 6)
                ft_hi(g + 1, 7)
                agg_out(g - 1, 3)
                mish_blocks(g, KC)

            def last_group():
                g = NG - 1
                mish_blocks(g, 0, before_last=lambda: z_hi(g - 1, 0))
                z_hi(g - 1, 1)
                xt_hi(0, 0, 0)
                xt_hi(0, 0, 1)
                act.wait_ge(loaded_w3a, 16)
                for c in range(KC):
                    weight_hi(w3a[0][:, c, :], w34_in[:, c, :])
                mish_exp(g, KC)
                agg_out(g - 1, 0)
                agg_out(g - 1, 1)
                mish_inverse(KC % 2, GE, NB * g + KC)
                mish_exp(g, KC + 1)
                mish_hi(g, KC)
                mish_inverse((KC + 1) % 2, GE, NB * g + KC + 1)
                mish_hi(g, KC + 1)
                z_hi(g - 1, 2)
                z_hi(g - 1, 3)
                mish_exp(g, KC + 2)
                agg_out(g - 1, 2)
                agg_out(g - 1, 3)
                mish_inverse((KC + 2) % 2, GE, NB * g + KC + 2)
                mish_exp(g, KC + 3)
                mish_hi(g, KC + 2)
                mish_inverse((KC + 3) % 2, GE, NB * g + KC + 3)
                mish_hi(g, KC + 3)

            def last_rows():
                g = NG - 1
                z_hi(g, 0)
                z_hi(g, 1)
                agg_out(g, 0)
                xt_hi(0, 0, 2)
                z_hi(g, 2)
                agg_out(g, 1)
                xt_hi(0, 0, 3)
                z_hi(g, 3)
                agg_out(g, 2)
                agg_out(g, 3)
                act.wait_ge(loaded_w4, 16)
                for c in range(KC):
                    weight_hi(w4[0][:, c, :], w34_in[:, KC + c, :])

            act.preload_act_table_set("natural_log_exp_and_others")
            act.wait_ge(loaded_w1a, 16)
            for c in range(KC):
                weight_hi(w1[0][:, c, :], w1_in[:, c, :])
            for c in range(KC):
                ft_hi(0, c)
            act.wait_ge(loaded_w1b, 16)
            for c in range(KC, XC):
                weight_hi(w1[0][:, c, :], w1_in[:, c, :])
            for c in range(KC, XC - 2):
                ft_hi(0, c)
            act.wait_ge(loaded_w1e, 32)
            weight_hi(w1e[0], w1e_in)
            act.wait_ge(loaded_w2, 16)
            for c in range(KC):
                weight_hi(w2[0][:, c, :], w2_in[:, c, :])
            for c in range(XC - 2, XC):
                ft_hi(0, c)
            act.wait_ge(loaded_w3b, 16)
            for c in range(KC):
                weight_hi(w3b[0][:, c, :], w3b_in[:, c, :])
            act.wait_ge(loaded_bias, 32)
            act.wait_ge(constants_made, 5)
            act.wait_ge(w_split, XC + 1 + 2 * KC)

            M0 = NB * NG

            def xt_hi(a, b, k):
                act.wait_ge(turned_node, a + k + 1)
                if past(a + k - 1):
                    act.wait_ge(w3_done, a + k - 1)
                act.activation(xt[0][:, k % 2].rearrange("p c n -> p (c n)"), ps[:, TURN + k % 2, :],
                               ACT.Copy).then_inc(xt_hi_ready, 1)

            def ut_hi(a, b, k):
                act.wait_ge(turned_u, a + k + 1)
                if past(a + k - 1):
                    act.wait_ge(w4_done, a + k - 1)
                act.activation(ut[0][:, k % 2].rearrange("p c n -> p (c n)"), ps[:, BLOCK + 2 + k % 2, :],
                               ACT.Copy).then_inc(ut_hi_ready, 1)

            def node_exp(a, b, k):
                act.wait_ge(v_ready, a + k + 1)
                act.wait_ge(mish_ready, M0 + a + k - 1)
                act.activation(e_buf[:, k % 2, :], v_row[:, k % RING, :], ACT.Exp).then_inc(e_ready, 1)

            def node_square(a, b, k):
                act.wait_ge(e_held, M0 + a + k + 1)
                act.wait_ge(mish_ready, M0 + a + k - 1)
                act.activation(n_buf[:, k % 2, :], e_buf[:, k % 2, :], ACT.Square).then_inc(n_ready, 1)

            def node_ln(a, b, k):
                act.wait_ge(n_ready, M0 + a + k + 1)
                act.activation(e_buf[:, k % 2, :], n_buf[:, k % 2, :], ACT.Ln, bias=1.0).then_inc(ln_done, 1)

            def node_inverse(a, b, k):
                act.wait_ge(ln_done, M0 + a + k + 1)
                act.activation(e_buf[:, k % 2, :], e_buf[:, k % 2, :], ACT.Exp, scale=-1.0).then_inc(inv_ready, 1)

            def squares_y(a, b, k):
                q = k % RING
                act.wait_ge(nmean1_ready, a + k + 1)
                if past(a + k):
                    act.wait_ge(squared1, a + k)
                act.activation(unused[:, 0, :], y_row[:, q, :], ACT.Square, bias=nmean1[:, q:q + 1],
                               accum_out=ssq1[:, q:q + 1]).then_inc(squared1, 1)

            def squares_w(a, b, k):
                q = k % RING
                act.wait_ge(nmean2_ready, a + k + 1)
                if past(a + k):
                    act.wait_ge(squared2, a + k)
                act.activation(unused[:, 1, :], w_row[:, k % 2, :], ACT.Square, bias=nmean2[:, q:q + 1],
                               accum_out=ssq2[:, q:q + 1]).then_inc(squared2, 1)

            def final(a, b, k):
                q = k % RING
                act.wait_ge(shift2_ready, a + k + 1)
                if past(16 * (b + k // RING)):
                    act.wait_ge(stored[q], 16 * (b + k // RING))
                act.activation(o_row[:, q, :], w_row[:, k % 2, :], ACT.Identity, bias=shift2[:, q:q + 1],
                               scale=rstd2[:, q:q + 1]).then_inc(normed, 1)

            def step(a, b, k, live):
                if live(a, k - 5):
                    final(a, b, k - 5)
                if live(a, k - 1):
                    node_exp(a, b, k - 1)
                if live(a, k + 1) and not ahead(a, k + 1):
                    xt_hi(a, b, k + 1)
                if live(a, k - 1):
                    node_square(a, b, k - 1)
                    node_ln(a, b, k - 1)
                if live(a, k - 4):
                    squares_w(a, b, k - 4)
                if live(a, k - 1):
                    node_inverse(a, b, k - 1)
                if live(a, k - 3):
                    squares_y(a, b, k - 3)
                if live(a, k - 2):
                    ut_hi(a, b, k - 2)

            first_group()
            group(1)
            with act.Fori(2, NG - 1) as g:
                group(g)
            last_group()
            last_rows()
            run_steps(act, step, 1)

        @block.vector
        def _(dve):
            def weight_lo(i, out_, in_, hi):
                dve.wait_ge(w_hi_ready, i + 1)
                dve.tensor_tensor(out_, in_, hi.bitcast(F32), ALU.subtract).then_inc(w_split, 1)

            def mish_n(slot, width, i):
                e = e_buf[:, slot, 0:width]
                dve.wait_ge(e_ready, i + 1)
                dve.tensor_scalar(e, e, E_MAX, None, ALU.min).then_inc(e_held, 1)
                dve.wait_ge(e_held, i + 1)
                if past(i - 1):
                    dve.wait_ge(mish_ready, i - 1)
                dve.scalar_tensor_tensor(out=n_buf[:, slot, 0:width], in0=e, scalar=2.0, in1=e,
                                         op0=ALU.add, op1=ALU.mult).then_inc(n_ready, 1)

            def block_vn(g, b):
                i = NB * g + b
                bias = (b1_col if b < KC else b2_col)[:, b % KC:b % KC + 1]
                dve.wait_ge(n_ready, i + 1)
                dve.wait_ge(ln_done, i + 1)
                dve.scalar_tensor_tensor(out=n_buf[:, b % 2, 0:GE], in0=ps[:, BLOCK + b % KC, 0:GE], scalar=bias,
                                         in1=n_buf[:, b % 2, 0:GE], op0=ALU.add, op1=ALU.mult).then_inc(vn_ready, 1)

            def mish_f(slot, width, i):
                dve.wait_ge(inv_ready, i + 1)
                dve.wait_ge(vn_ready, i + 1)
                dve.tensor_tensor(f_buf[:, slot, 0:width], n_buf[:, slot, 0:width], e_buf[:, slot, 0:width],
                                  ALU.mult).then_inc(mish_ready, 1)

            def block_lo(g, b):
                i = NB * g + b
                t = ht if b < KC else mt
                dve.wait_ge(mish_hi_ready, i + 1)
                dve.tensor_tensor(t[1][:, b % KC, :], f_buf[:, b % 2, 0:GE], t[0][:, b % KC, :].bitcast(F32),
                                  ALU.subtract).then_inc(mish_split, 1)

            def mish_blocks(g, first_block, n=KC, before_last=None, after_n=None):
                for b in range(first_block, first_block + n):
                    mish_n(b % 2, GE, NB * g + b)
                    if b > first_block:
                        block_lo(g, b - 1)
                    if after_n:
                        after_n(b)
                    block_vn(g, b)
                    if past(NB * g + b - 1):
                        mish_split_before = NB * g + b - 1
                        dve.wait_ge(mish_hi_ready, mish_split_before)
                        dve.wait_ge(mish_split, mish_split_before)
                    mish_f(b % 2, GE, NB * g + b)
                if before_last:
                    before_last()
                block_lo(g, first_block + n - 1)

            def ft_lo(g, c):
                dve.wait_ge(ft_hi_ready, XC * g + c + 1)
                dve.tensor_tensor(ft[1][:, c, :], ps[:, TURN + c % 2, 0:GE], ft[0][:, c, :].bitcast(F32),
                                  ALU.subtract).then_inc(ft_split, 1)

            def ea_out(g):
                dve.wait_ge(turned_ea, g + 1)
                dve.tensor_copy(eat, ps[:, TURN, 0:GE]).then_inc(eat_ready, 1)

            def ea_split(g):
                rows = ea_all[0:LE, bass.ds(g * GT, GT), :]
                if past(g):
                    dve.wait_ge(turned_ea, g)
                dve.tensor_copy(ea_cat[0:LE, :, 0:D], rows).then_inc(ea_hi_ready, 1)
                dve.wait_ge(ea_hi_ready, g + 1)
                dve.tensor_tensor(ea_cat[0:LE, :, D:2 * D], rows, ea_cat[0:LE, :, 0:D].bitcast(F32),
                                  ALU.subtract).then_inc(ea_cat_ready, 1)

            def z_lo(g, j):
                dve.wait_ge(z_hi_ready, GT * g + j + 1)
                dve.tensor_tensor(zs[1][0:LE, j % 2, :], ps[0:LE, ROWS + j % 2, :], zs[0][0:LE, j % 2, :].bitcast(F32),
                                  ALU.subtract).then_inc(z_split, 1)

            def same_dst(g):
                dve.wait_ge(turned_dst, g + 1)
                if past(GT * g):
                    dve.wait_ge(sum_done, GT * g)
                for j in range(GT):
                    dve.tensor_scalar(same[0:LE, j, :], ps[0:LE, TURN + 1, j * LE:(j + 1) * LE],
                                      dst_sum[0:LE, j:j + 1], None, ALU.is_equal).then_inc(same_part_ready, 1)
                dve.wait_ge(same_part_ready, GT * (g + 1))
                dve.tensor_tensor(same_below[0:LE], same[0:LE].bitcast(F32),
                                  below[0:LE].rearrange("p (a n) -> p a n", a=1).to_broadcast([LE, GT, LE]),
                                  ALU.mult).then_inc(same_ready, 1)
                dve.wait_ge(same_ready, g + 1)
                dve.tensor_reduce(n_before[0:LE, :], same_below[0:LE], AX.X, ALU.add).then_inc(counted, 1)
                if past(g):
                    dve.wait_ge(add_row_ready, g)
                dve.tensor_scalar(to_unread, dst_sum, unread_f, -1.0, ALU.subtract, ALU.mult).then_inc(distance, 1)
                dve.wait_ge(counted, g + 1)
                dve.wait_ge(distance, g + 1)
                dve.scalar_tensor_tensor(out=to_unread, in0=n_before, scalar=1.0, in1=to_unread, op0=ALU.min,
                                         op1=ALU.mult).then_inc(moved, 1)
                dve.wait_ge(moved, g + 1)
                if past(16 * GT * g):
                    dve.wait_ge(added, 16 * GT * g)
                dve.tensor_tensor(add_row, to_unread, dst_sum, ALU.add).then_inc(add_row_ready, 1)

            def take_dst(g):
                if past(g):
                    dve.wait_ge(add_row_ready, g)
                dve.tensor_copy(dst_sum, dst_f[:, bass.ds(g * GT, GT)]).then_inc(dst_sum_ready, 1)

            def first_group():
                def more(b):
                    for c in (2 * (b - KC) + 4, 2 * (b - KC) + 5):
                        if c < XC:
                            ft_lo(1, c)

                take_dst(0)
                mish_blocks(0, 0, before_last=lambda: ft_lo(1, 0))
                for c in range(1, 4):
                    ft_lo(1, c)
                dve.wait_ge(loaded_ea_rest, 16)
                ea_split(1)
                mish_blocks(0, KC, after_n=more)
                ea_out(1)

            def group(g):
                def before_last():
                    z_lo(g - 1, 0)
                    ft_lo(g + 1, 0)

                same_dst(g - 1)
                take_dst(g)
                ea_split(g + 1)
                mish_blocks(g, 0, before_last=before_last)
                ft_lo(g + 1, 1)
                z_lo(g - 1, 1)
                ft_lo(g + 1, 2)
                ft_lo(g + 1, 3)
                z_lo(g - 1, 2)
                ft_lo(g + 1, 4)
                ft_lo(g + 1, 5)
                z_lo(g - 1, 3)
                ft_lo(g + 1, 6)
                ft_lo(g + 1, 7)
                ea_out(g + 1)
                mish_blocks(g, KC)

            def last_group():
                g = NG - 1
                same_dst(g - 1)
                take_dst(g)
                mish_blocks(g, 0, before_last=lambda: z_lo(g - 1, 0))
                z_lo(g - 1, 1)
                xt_lo(0, 0, 0)
                xt_lo(0, 0, 1)
                for c in range(KC):
                    weight_lo(XC + 1 + 2 * KC + c, w3a[1][:, c, :], w34_in[:, c, :], w3a[0][:, c, :])
                mish_blocks(g, KC, 2)
                z_lo(g - 1, 2)
                z_lo(g - 1, 3)
                mish_blocks(g, KC + 2, 2)

            def last_rows():
                g = NG - 1
                same_dst(g)
                z_lo(g, 0)
                z_lo(g, 1)
                xt_lo(0, 0, 2)
                z_lo(g, 2)
                xt_lo(0, 0, 3)
                z_lo(g, 3)
                for c in range(KC):
                    weight_lo(XC + 1 + 3 * KC + c, w4[1][:, c, :], w34_in[:, KC + c, :], w4[0][:, c, :])

            def w1_lo(c):
                weight_lo(c, w1[1][:, c, :], w1_in[:, c, :], w1[0][:, c, :])

            for c in range(KC):
                w1_lo(c)
            dve.wait_ge(loaded_ea_first, 16)
            ea_split(0)
            for c in range(KC):
                ft_lo(0, c)
            for c in range(KC, XC):
                w1_lo(c)
            for c in range(KC, XC - 2):
                ft_lo(0, c)
            weight_lo(XC, w1e[1], w1e_in, w1e[0])
            for c in range(KC):
                weight_lo(XC + 1 + c, w2[1][:, c, :], w2_in[:, c, :], w2[0][:, c, :])
            for c in range(XC - 2, XC):
                ft_lo(0, c)
            ea_out(0)
            for c in range(KC):
                weight_lo(XC + 1 + KC + c, w3b[1][:, c, :], w3b_in[:, c, :], w3b[0][:, c, :])
            dve.wait_ge(loaded_pad, 16)
            dve.wait_ge(unread_set, 1)
            dve.tensor_copy(dst_f, dst_pad).then_inc(dst_float, 1)
            dve.tensor_copy(unread_f, unread_i).then_inc(dst_float, 1)
            dve.wait_ge(loaded_bias, 32)
            dve.wait_ge(dst_float, 2)
            dve.wait_ge(constants_made, 5)

            M0 = NB * NG

            def xt_lo(a, b, k):
                dve.wait_ge(xt_hi_ready, a + k + 1)
                dve.tensor_tensor(xt[1][:, k % 2].rearrange("p c n -> p (c n)"), ps[:, TURN + k % 2, :],
                                  xt[0][:, k % 2].rearrange("p c n -> p (c n)").bitcast(F32),
                                  ALU.subtract).then_inc(xt_split, 1)

            def ut_lo(a, b, k):
                dve.wait_ge(ut_hi_ready, a + k + 1)
                dve.tensor_tensor(ut[1][:, k % 2].rearrange("p c n -> p (c n)"), ps[:, BLOCK + 2 + k % 2, :],
                                  ut[0][:, k % 2].rearrange("p c n -> p (c n)").bitcast(F32),
                                  ALU.subtract).then_inc(ut_split, 1)

            def add_pre(a, b, k):
                q = k % RING
                dve.wait_ge(w3_done, a + k + 1)
                dve.wait_ge(pre_in[q], 16 * (b + k // RING + 1))
                dve.tensor_tensor(v_row[:, q, :], ps[:, w3_bank(a, k), :], v_row[:, q, :], ALU.add).then_inc(v_ready, 1)

            def node_held(a, b, k):
                e = e_buf[:, k % 2, :]
                dve.wait_ge(e_ready, M0 + a + k + 1)
                dve.tensor_scalar(e, e, E_MAX, 1.0, ALU.min, ALU.add).then_inc(e_held, 1)

            def node_vn(a, b, k):
                q = k % RING
                dve.wait_ge(n_ready, M0 + a + k + 1)
                dve.scalar_tensor_tensor(out=v_row[:, q, :], in0=n_buf[:, k % 2, :], scalar=-1.0, in1=v_row[:, q, :],
                                         op0=ALU.add, op1=ALU.mult).then_inc(vn_ready, 1)

            def node_f(a, b, k):
                dve.wait_ge(inv_ready, M0 + a + k + 1)
                dve.wait_ge(vn_ready, M0 + a + k + 1)
                if past(a + k - 1):
                    dve.wait_ge(turned_u, a + k - 1)
                dve.tensor_tensor(f_buf[:, k % 2, :], v_row[:, k % RING, :], e_buf[:, k % 2, :],
                                  ALU.mult).then_inc(mish_ready, 1)

            def residual(a, b, k):
                q = k % RING
                dve.wait_ge(w4_done, a + k + 1)
                dve.wait_ge(x_b4, a + k + 1)
                dve.scalar_tensor_tensor(out=y_row[:, q, :], in0=ps[:, ROWS + k % 2, :], scalar=1.0, in1=y_row[:, q, :],
                                         op0=ALU.mult, op1=ALU.add,
                                         accum_out=sum1[:, q:q + 1]).then_inc(y_ready, 1)

            def norm_gamma(a, b, k):
                q = k % RING
                dve.wait_ge(nmean1_ready, a + k + 1)
                dve.wait_ge(squared1, a + k + 1)
                dve.scalar_tensor_tensor(out=y_row[:, q, :], in0=y_row[:, q, :], scalar=nmean1[:, q:q + 1],
                                         in1=gamma_row, op0=ALU.add, op1=ALU.mult).then_inc(y_gamma_ready, 1)

            def residual2(a, b, k):
                q = k % RING
                dve.wait_ge(rstd1_ready, a + k + 1)
                if past(a + k - 1):
                    dve.wait_ge(normed, a + k - 1)
                dve.wait_ge(y_gamma_ready, a + k + 1)
                dve.wait_ge(x_beta, a + k + 1)
                dve.scalar_tensor_tensor(out=w_row[:, k % 2, :], in0=y_row[:, q, :], scalar=rstd1[:, q:q + 1],
                                         in1=xb_row[:, q, :], op0=ALU.mult, op1=ALU.add,
                                         accum_out=sum2[:, q:q + 1]).then_inc(w_ready, 1)

            def step(a, b, k, live):
                if live(a, k - 1) and not (ahead(a, k - 1) and k > 2):
                    add_pre(a, b, k - 1)
                if isinstance(a, int) and k == 2:
                    for early in range(2, AHEAD):
                        add_pre(0, 0, early)
                if live(a, k - 4):
                    norm_gamma(a, b, k - 4)
                if live(a, k - 1):
                    node_held(a, b, k - 1)
                if live(a, k - 4):
                    residual2(a, b, k - 4)
                if live(a, k + 1) and not ahead(a, k + 1):
                    xt_lo(a, b, k + 1)
                if live(a, k - 3):
                    residual(a, b, k - 3)
                if live(a, k - 1):
                    node_vn(a, b, k - 1)
                    node_f(a, b, k - 1)
                if live(a, k - 2):
                    ut_lo(a, b, k - 2)

            first_group()
            group(1)
            with dve.Fori(2, NG - 1) as g:
                group(g)
            last_group()
            last_rows()
            dve.wait_ge(loaded_rows, 48)
            dve.wait_ge(mish_hi_ready, M0)
            dve.wait_ge(mish_split, M0)
            run_steps(dve, step, 1)


_INS = ["x", "src", "dst", "edge_attr_64"] + [
    f"L0_gnn_{n}" for n in ("W1", "b1", "W2", "b2", "W3", "b3", "W4", "b4", "gamma", "beta")]


def kernel(**inputs):
    import numpy as np
    import concourse.bacc as bacc
    from concourse.bass_utils import run_bass_kernel_spmd

    nc = bacc.Bacc("TRN2", target_bir_lowering=False, num_devices=1)
    arrays, args = {}, []
    for name in _INS:
        a = np.ascontiguousarray(inputs[name])
        arrays[f"in_{name}"] = a
        args.append(nc.dram_tensor(f"in_{name}", a.shape, mybir.dt.from_np(a.dtype), kind="ExternalInput").ap())
    out = nc.dram_tensor("out_rows", inputs["x"].shape, F32, kind="ExternalOutput").ap()
    gnn_kernel(nc, *args, out)
    r = run_bass_kernel_spmd(nc, [arrays], core_ids=[0])
    return r.results[0]["out_rows"]
```

```python
import concourse.bass as bass
from concourse import mybir

ACT = mybir.ActivationFunctionType
ALU = mybir.AluOpType
AX = mybir.AxisListType
F32 = mybir.dt.float32
F32R = mybir.dt.float32r
I32 = mybir.dt.int32
BF16 = mybir.dt.bfloat16

P = 128
E_MAX = float(2 ** 14)
EPS = 1e-5
RING = 4


def gnn_kernel(nc, x, src, dst, edge_attr, W1, b1, W2, b2, W3, b3, W4, b4, gamma, beta, out):
    N, H = x.shape
    E, D = edge_attr.shape
    KC = H // P
    LE = 125
    ET = E // LE
    GT = 4
    NG = ET // GT
    GE = GT * LE
    XC = 2 * KC
    NB = 2 * KC
    NT = -(-N // P)
    PIECE = 4
    PIECES = -(-(NT + 1) // PIECE)
    AHEAD = 6
    WARM = 18
    LAST = N - P
    PT = NT + 1
    assert LE * ET == E and NG * GT == ET and 2 * D == P and KC == GT == RING == 4 and NG >= 4

    pre = nc.dram_tensor("pre_table", (PT * P, H), F32).ap()

    start = -(-nc.sbuf_base // 64) * 64
    end = nc.sbuf_usable_end
    at = [start]

    def place(name, shape, dt, offset=None):
        size = 2 if dt == BF16 else 4
        for n in shape[1:]:
            size *= n
        if offset is None:
            offset = at[0]
            at[0] += -(-size // 32) * 32
        assert offset + size <= end, name
        return nc.alloc_sbuf_tensor_at(name, shape, dt, offset=offset).ap()

    ident = place("ident", [P, P], F32)
    below = place("below", [P, LE], F32)
    b1_col = place("b1_col", [P, KC], F32)
    b2_col = place("b2_col", [P, KC], F32)
    b3_row = place("b3_row", [P, H], F32)
    b4_row = place("b4_row", [P, H], F32)
    gamma_row = place("gamma_row", [P, H], F32)
    beta_row = place("beta_row", [P, H], F32)
    src_all = place("src_all", [P, ET], I32)
    dst_all = place("dst_all", [P, ET], I32)
    dst_pad = place("dst_pad", [P, ET], I32)
    dst_f = place("dst_f", [P, ET], F32)
    unread_i = place("unread_i", [P, 1], I32)
    unread_f = place("unread_f", [P, 1], F32)
    src_now = place("src_now", [P, GT], I32)
    dst_now = place("dst_now", [P, GT], I32)
    dst_sum = place("dst_sum", [P, GT], F32)
    n_before = place("n_before", [P, GT], F32)
    to_unread = place("to_unread", [P, GT], F32)
    add_row = place("add_row", [P, GT], I32)
    minus_half = place("minus_half", [P, 1], F32)
    sum1, nmean1, ssq1, var1, rstd1 = (place(k + "1", [P, RING], F32) for k in ("sum", "nmean", "ssq", "var", "rstd"))
    sum2, nmean2, ssq2, var2, rstd2 = (place(k + "2", [P, RING], F32) for k in ("sum", "nmean", "ssq", "var", "rstd"))
    shift2 = place("shift2", [P, RING], F32)
    e_buf = place("e_buf", [P, 2, H], F32)
    n_buf = place("n_buf", [P, 2, H], F32)
    f_buf = place("f_buf", [P, 2, H], F32)
    w2 = [place(f"w2_{s}", [P, KC, H], F32R) for s in ("hi", "lo")]
    w3b = [place(f"w3b_{s}", [P, KC, H], F32R) for s in ("hi", "lo")]
    at_w1 = at[0]
    w1 = [place(f"w1_{s}", [P, XC, H], F32R) for s in ("hi", "lo")]
    w1e = [place(f"w1e_{s}", [P, H], F32R) for s in ("hi", "lo")]
    at_ft = at[0]
    ft = [place(f"ft_{s}", [P, XC, GE], F32R) for s in ("hi", "lo")]
    eat = place("eat", [P, GE], F32R)
    at_xg = at[0]
    xg = place("xg", [P, 2 * GT, H], F32)
    at_h = at[0]
    ht = [place(f"ht_{s}", [P, KC, GE], F32R) for s in ("hi", "lo")]
    mt = [place(f"mt_{s}", [P, KC, GE], F32R) for s in ("hi", "lo")]
    same = place("same", [P, GT, LE], F32R)
    same_below = place("same_below", [P, GT, LE], F32)
    at_ea = at[0]
    ea_cat = place("ea_cat", [P, GT, P], F32R)
    at_z = at[0]
    zs = [place(f"z_{s}", [P, 2, H], F32R) for s in ("hi", "lo")]
    agg = place("agg", [P, GT, H], F32)
    ea_all = place("ea_all", [P, ET, D], F32)
    at_end = at[0]

    w1_in = place("w1_in", [P, XC, H], F32, at_h)
    w2_in = place("w2_in", [P, KC, H], F32, at_h + XC * H * 4)
    w3b_in = place("w3b_in", [P, KC, H], F32, at_h + (XC + KC) * H * 4)
    w1e_in = place("w1e_in", [P, H], F32, at_z)
    assert at_h + (XC + 2 * KC) * H * 4 <= at_ea and 2 * KC * GE * 4 <= (XC + KC) * H * 4

    w3a = [place(f"w3a_{s}", [P, KC, H], F32R, at_w1 + i * KC * H * 4) for i, s in enumerate(("hi", "lo"))]
    w4 = [place(f"w4_{s}", [P, KC, H], F32R, at_w1 + (2 + i) * KC * H * 4) for i, s in enumerate(("hi", "lo"))]
    w34_in = place("w34_in", [P, 2 * KC, H], F32, at_xg)
    at[0] = at_ft
    xt = [place(f"xt_{s}", [P, 2, KC, P], F32R) for s in ("hi", "lo")]
    x_row = place("x_row", [P, AHEAD, H], F32)
    y_row = place("y_row", [P, AHEAD, H], F32)
    assert at[0] <= at_xg
    at[0] = at_h
    xb_row = place("xb_row", [P, AHEAD, H], F32)
    assert at[0] <= at_h + 2 * KC * GE * 4
    ut = [place(f"ut_{s}", [P, 2, KC, P], F32R) for s in ("hi", "lo")]
    w_row = place("w_row", [P, 2, H], F32)
    v_row = place("v_row", [P, AHEAD, H], F32)
    o_row = place("o_row", [P, RING, H], F32)
    unused = place("unused", [P, 2, H], BF16)
    assert at[0] <= at_end

    ps = nc.alloc_psum_tensor("ps", [P, 8, H], F32).ap()
    BLOCK, TURN, ROWS = 0, 4, 6

    pads_set = nc.alloc_semaphore("pads_set")
    loaded_src = nc.alloc_semaphore("loaded_src")
    loaded_dst = nc.alloc_semaphore("loaded_dst")
    loaded_pad = nc.alloc_semaphore("loaded_pad")
    loaded_ea_first = nc.alloc_semaphore("loaded_ea_first")
    loaded_ea_rest = nc.alloc_semaphore("loaded_ea_rest")
    loaded_w1a = nc.alloc_semaphore("loaded_w1a")
    loaded_w1b = nc.alloc_semaphore("loaded_w1b")
    loaded_w1e = nc.alloc_semaphore("loaded_w1e")
    loaded_w2 = nc.alloc_semaphore("loaded_w2")
    loaded_w3b = nc.alloc_semaphore("loaded_w3b")
    loaded_w3a = nc.alloc_semaphore("loaded_w3a")
    loaded_w4 = nc.alloc_semaphore("loaded_w4")
    loaded_bias = nc.alloc_semaphore("loaded_bias")
    loaded_b3 = nc.alloc_semaphore("loaded_b3")
    loaded_rows = nc.alloc_semaphore("loaded_rows")
    ident_made = nc.alloc_semaphore("ident_made")
    constants_made = nc.alloc_semaphore("constants_made")
    unread_set = nc.alloc_semaphore("unread_set")
    dst_float = nc.alloc_semaphore("dst_float")
    w_hi_ready = nc.alloc_semaphore("w_hi_ready")
    w_split = nc.alloc_semaphore("w_split")
    table_set = [nc.alloc_semaphore(f"table_set{i}") for i in range(2)]
    added = nc.alloc_semaphore("added")
    src_staged = nc.alloc_semaphore("src_staged")
    dst_staged = nc.alloc_semaphore("dst_staged")
    turned_x = nc.alloc_semaphore("turned_x")
    ft_hi_ready = nc.alloc_semaphore("ft_hi_ready")
    ft_split = nc.alloc_semaphore("ft_split")
    ea_hi_ready = nc.alloc_semaphore("ea_hi_ready")
    ea_cat_ready = nc.alloc_semaphore("ea_cat_ready")
    turned_ea = nc.alloc_semaphore("turned_ea")
    eat_ready = nc.alloc_semaphore("eat_ready")
    block_done = nc.alloc_semaphore("block_done")
    e_ready = nc.alloc_semaphore("e_ready")
    e_held = nc.alloc_semaphore("e_held")
    n_ready = nc.alloc_semaphore("n_ready")
    ln_done = nc.alloc_semaphore("ln_done")
    inv_ready = nc.alloc_semaphore("inv_ready")
    vn_ready = nc.alloc_semaphore("vn_ready")
    mish_ready = nc.alloc_semaphore("mish_ready")
    mish_hi_ready = nc.alloc_semaphore("mish_hi_ready")
    mish_split = nc.alloc_semaphore("mish_split")
    z_done = nc.alloc_semaphore("z_done")
    z_hi_ready = nc.alloc_semaphore("z_hi_ready")
    z_split = nc.alloc_semaphore("z_split")
    sum_done = nc.alloc_semaphore("sum_done")
    agg_ready = nc.alloc_semaphore("agg_ready")
    dst_sum_ready = nc.alloc_semaphore("dst_sum_ready")
    turned_dst = nc.alloc_semaphore("turned_dst")
    same_part_ready = nc.alloc_semaphore("same_part_ready")
    same_ready = nc.alloc_semaphore("same_ready")
    counted = nc.alloc_semaphore("counted")
    distance = nc.alloc_semaphore("distance")
    moved = nc.alloc_semaphore("moved")
    add_row_ready = nc.alloc_semaphore("add_row_ready")
    turned_node = nc.alloc_semaphore("turned_node")
    xt_hi_ready = nc.alloc_semaphore("xt_hi_ready")
    xt_split = nc.alloc_semaphore("xt_split")
    w3_done = nc.alloc_semaphore("w3_done")
    v_ready = nc.alloc_semaphore("v_ready")
    turned_u = nc.alloc_semaphore("turned_u")
    ut_hi_ready = nc.alloc_semaphore("ut_hi_ready")
    ut_split = nc.alloc_semaphore("ut_split")
    w4_done = nc.alloc_semaphore("w4_done")
    x_b4 = nc.alloc_semaphore("x_b4")
    x_beta = nc.alloc_semaphore("x_beta")
    y_ready = nc.alloc_semaphore("y_ready")
    nmean1_ready = nc.alloc_semaphore("nmean1_ready")
    squared1 = nc.alloc_semaphore("squared1")
    var1_ready = nc.alloc_semaphore("var1_ready")
    rstd1_ready = nc.alloc_semaphore("rstd1_ready")
    y_gamma_ready = nc.alloc_semaphore("y_gamma_ready")
    w_ready = nc.alloc_semaphore("w_ready")
    nmean2_ready = nc.alloc_semaphore("nmean2_ready")
    squared2 = nc.alloc_semaphore("squared2")
    var2_ready = nc.alloc_semaphore("var2_ready")
    rstd2_ready = nc.alloc_semaphore("rstd2_ready")
    shift2_ready = nc.alloc_semaphore("shift2_ready")
    normed = nc.alloc_semaphore("normed")
    src_in = [nc.alloc_semaphore(f"src_in{j}") for j in range(GT)]
    dst_in = [nc.alloc_semaphore(f"dst_in{j}") for j in range(GT)]
    x_in = [nc.alloc_semaphore(f"x_in{j}") for j in range(RING)]
    pre_in = [nc.alloc_semaphore(f"pre_in{j}") for j in range(RING)]
    stored = [nc.alloc_semaphore(f"stored{j}") for j in range(RING)]

    def past(count):
        return not isinstance(count, int) or count > 0

    def split_matmul(pe, out_, lhs, rhs, first, last):
        pe.matmul(out_, lhs[0], rhs[0], start=first, stop=False)
        pe.matmul(out_, lhs[0], rhs[1], start=False, stop=False)
        return pe.matmul(out_, lhs[1], rhs[0], start=False, stop=last)

    def ahead(a, k):
        return isinstance(a, int) and a + k < AHEAD

    def early(a, k):
        return isinstance(a, int) and a + k < AHEAD

    def lone(a, k, stage):
        return isinstance(a, int) and a + k == NT - 1 + stage

    def over(a, k):
        return isinstance(a, int) and a + k > NT

    def w3_bank(a, k):
        if ahead(a, k):
            return BLOCK + k if k < 4 else ROWS + k - 4
        return BLOCK + k % 2

    def slot(a, k):
        return k if ahead(a, k) else k % RING

    def z_bank(g, j):
        return BLOCK + j if isinstance(g, int) and g == NG - 1 and j >= 2 else ROWS + j % 2

    def run_steps(eng, step, begin):
        first, end = 3, (NT - 2 - 3 - (RING - 1)) // RING + 1
        inside = lambda a, k: 0 <= a + k < NT
        for k in range(begin, RING * first):
            step(0, 0, k, inside)
        with eng.Fori(first, end) as b:
            for k in range(RING):
                step(RING * b, b, k, lambda a, k: True)
        for k in range(RING * end, NT + 6):
            step(0, 0, k, inside)

    with nc.Block() as block:

        @block.sync
        def _(sp):
            def row(v):
                return v.rearrange("(a d) -> a d", a=1).to_broadcast([P, H])

            sp.wait_ge(pads_set, 3)
            sp.dma_start(src_all[0:LE, :], src.rearrange("(p t) -> p t", t=ET)).then_inc(loaded_src, 16)
            sp.dma_start(dst_all[0:LE, :], dst.rearrange("(p t) -> p t", t=ET)).then_inc(loaded_dst, 16)
            ea_rows = edge_attr.rearrange("(p t) d -> p t d", t=ET)
            w1_rows = W1[0:2 * H, :].rearrange("(c p) n -> p c n", p=P)
            sp.dma_start(w1_in[:, 0:KC, :], w1_rows[:, 0:KC, :]).then_inc(loaded_w1a, 16)
            sp.dma_start(ea_all[0:LE, 0:GT], ea_rows[:, 0:GT]).then_inc(loaded_ea_first, 16)
            sp.wait_ge(src_in[0], 16)
            sp.dma_start(w1_in[:, KC:XC, :], w1_rows[:, KC:XC, :]).then_inc(loaded_w1b, 16)
            for i in range(2):
                sp.dma_start(w1e_in[i * D:(i + 1) * D, :], W1[2 * H:2 * H + D, :]).then_inc(loaded_w1e, 16)
            sp.dma_start(b1_col, b1.rearrange("(c p) -> p c", p=P),
                         allow_slow_non_contiguous=True).then_inc(loaded_bias, 16)
            sp.dma_start(b2_col, b2.rearrange("(c p) -> p c", p=P),
                         allow_slow_non_contiguous=True).then_inc(loaded_bias, 16)
            sp.dma_start(dst_pad[0:LE, :], dst.rearrange("(p t) -> p t", t=ET)).then_inc(loaded_pad, 16)
            for j in range(GT):
                sp.wait_ge(dst_in[j], 16)
            sp.dma_start(w2_in, W2.rearrange("(c p) n -> p c n", p=P)).then_inc(loaded_w2, 16)
            sp.dma_start(ea_all[0:LE, GT:ET], ea_rows[:, GT:ET]).then_inc(loaded_ea_rest, 16)
            sp.dma_start(w3b_in, W3[H:2 * H, :].rearrange("(c p) n -> p c n", p=P)).then_inc(loaded_w3b, 16)
            sp.dma_start(b3_row, row(b3)).then_inc(loaded_b3, 16)
            sp.wait_ge(loaded_b3, 16)
            for i in range(PIECES):
                t, n = i * PIECE, min(PIECE, PT - i * PIECE)
                if i >= 2:
                    sp.wait_ge(table_set[i % 2], 16 * (i // 2))
                sp.dma_start(pre[t * P:(t + n) * P, :].rearrange("(n p) d -> p n d", p=P),
                             b3_row.rearrange("p (a d) -> p a d", a=1).to_broadcast([P, n, H])
                             ).then_inc(table_set[i % 2], 16)
            for tile_, v in ((b4_row, b4), (gamma_row, gamma), (beta_row, beta)):
                sp.dma_start(tile_, row(v)).then_inc(loaded_rows, 16)

            sp.wait_ge(turned_x, XC * NG)
            sp.dma_start(w34_in[:, 0:KC, :], W3[0:H, :].rearrange("(c p) n -> p c n", p=P)).then_inc(loaded_w3a, 16)
            sp.dma_start(w34_in[:, KC:2 * KC, :], W4.rearrange("(c p) n -> p c n", p=P)).then_inc(loaded_w4, 16)
            sp.wait_ge(block_done, NB * (NG - 1) + KC)

            def rows_of(a, b, k):
                t = a + k
                return slice(LAST, LAST + P) if isinstance(t, int) and t == NT - 1 else bass.ds(t * P, P)

            def load_x(a, b, k):
                if not ahead(a, k):
                    sp.wait_ge(turned_node, a + k - RING + 1)
                    sp.wait_ge(x_beta, a + k - RING + 1)
                elif k >= RING:
                    sp.wait_ge(x_in[k % RING], 16 * (k // RING))
                sp.dma_start(x_row[:, slot(a, k), :], x[rows_of(a, b, k), :]).then_inc(x_in[k % RING], 16)

            def load_pre(a, b, k):
                if not ahead(a, k):
                    sp.wait_ge(mish_ready, NB * NG + a + k - RING + 1)
                elif k >= RING:
                    sp.wait_ge(pre_in[k % RING], 16 * (k // RING))
                sp.dma_start(v_row[:, slot(a, k), :], pre[rows_of(a, b, k), :]).then_inc(pre_in[k % RING], 16)

            def store(a, b, k):
                sp.wait_ge(normed, a + k + 1)
                t = a + k
                if isinstance(t, int) and t == NT - 1:
                    skip = NT * P - N
                    sp.dma_start(out[LAST + skip:N, :], o_row[skip:P, k % RING, :]).then_inc(stored[k % RING], 16)
                else:
                    sp.dma_start(out[bass.ds(t * P, P), :], o_row[:, k % RING, :]).then_inc(stored[k % RING], 16)

            def step(a, b, k, live):
                if live(a, k + 3) and not ahead(a, k + 3):
                    load_x(a, b, k + 3)
                if live(a, k + 2) and not ahead(a, k + 2):
                    load_pre(a, b, k + 2)
                if live(a, k - 6):
                    store(a, b, k - 6)

            for k in range(AHEAD):
                load_x(0, 0, k)
            sp.wait_ge(added, 16 * ET)
            for k in range(AHEAD):
                load_pre(0, 0, k)
            run_steps(sp, step, 0)
            for j in range(RING):
                sp.wait_ge(stored[j], 16 * len(range(j, NT, RING)))

        @block.gpsimd
        def _(pool):
            pool.memset(src_all, 0).then_inc(pads_set, 1)
            pool.memset(dst_all, 0).then_inc(pads_set, 1)
            pool.iota(unread_i, [[0, 1]], base=NT * P, channel_multiplier=1).then_inc(unread_set, 1)
            pool.iota(dst_pad, [[0, ET]], base=NT * P, channel_multiplier=1).then_inc(pads_set, 1)

            def to_count(count):
                return count if isinstance(count, int) else pool.to_reg(count)


            def gather_src(g):
                if past(XC * (g - 1) + KC):
                    pool.wait_ge(turned_x, XC * (g - 1) + KC)
                pool.tensor_copy(src_now, src_all[:, bass.ds(g * GT, GT)]).then_inc(src_staged, 1)
                staged = to_count(g + 1)
                pool.wait_ge(pads_set, 3)
                pool.wait_ge(src_staged, staged)
                for j in range(GT):
                    pool.indirect_dma_start(
                        out=xg[:, j, :], out_offset=None, in_=x,
                        in_offset=bass.IndirectOffsetOnAxis(ap=src_now[:, j:j + 1], axis=0),
                    ).then_inc(src_in[j], 16)

            def gather_dst(g):
                if past(XC * g):
                    pool.wait_ge(turned_x, XC * g)
                pool.tensor_copy(dst_now, dst_all[:, bass.ds(g * GT, GT)]).then_inc(dst_staged, 1)
                staged = to_count(g + 1)
                pool.wait_ge(pads_set, 3)
                pool.wait_ge(dst_staged, staged)
                for j in range(GT):
                    pool.indirect_dma_start(
                        out=xg[:, GT + j, :], out_offset=None, in_=x,
                        in_offset=bass.IndirectOffsetOnAxis(ap=dst_now[:, j:j + 1], axis=0),
                    ).then_inc(dst_in[j], 16)

            def add_rows(g, j):
                chosen, summed, before = to_count(g + 1), to_count(GT * g + j + 1), to_count(16 * (GT * g + j))
                pool.wait_ge(pads_set, 3)
                pool.wait_ge(add_row_ready, chosen)
                pool.wait_ge(agg_ready, summed)
                if past(before):
                    pool.wait_ge(added, before)
                pool.indirect_dma_start(
                    out=pre, out_offset=bass.IndirectOffsetOnAxis(ap=add_row[:, j:j + 1], axis=0),
                    in_=agg[:, j, :], in_offset=None, compute_op=ALU.add,
                ).then_inc(added, 16)

            def group(g, last=False):
                add_rows(g - 1, 0)
                if not last:
                    gather_src(g + 2)
                add_rows(g - 1, 1)
                add_rows(g - 1, 2)
                if not last:
                    gather_dst(g + 2)
                add_rows(g - 1, 3)

            pool.memset(ident, 0.0).then_inc(ident_made, 1)
            pool.wait_ge(ident_made, 1)
            pool.affine_select(out=ident, in_=ident, compare_op=ALU.not_equal, fill=1.0, base=0,
                               pattern=[[-1, P]], channel_multiplier=1).then_inc(ident_made, 1)
            pool.wait_ge(pads_set, 3)
            pool.wait_ge(loaded_src, 16)
            gather_src(0)
            pool.wait_ge(loaded_dst, 16)
            gather_dst(0)
            gather_src(1)
            pool.memset(below, 1.0).then_inc(constants_made, 1)
            pool.memset(minus_half, -0.5).then_inc(constants_made, 1)
            pool.memset(n_before, 0.0).then_inc(constants_made, 1)
            pool.memset(agg, 0.0).then_inc(constants_made, 1)
            pool.wait_ge(constants_made, 4)
            pool.affine_select(out=below, in_=below, compare_op=ALU.is_gt, fill=0.0, base=0,
                               pattern=[[-1, LE]], channel_multiplier=1).then_inc(constants_made, 1)
            gather_dst(1)
            for g in (2, 3):
                gather_src(g)
                gather_dst(g)
            for i in range(2):
                pool.wait_ge(table_set[i], 16 * len(range(i, PIECES, 2)))
            for j in range(GT):
                add_rows(0, j)
            with pool.Fori(2, NG - 2) as g:
                group(g)
            group(NG - 2, last=True)
            group(NG - 1, last=True)

            def x_plus(a, b, k):
                pool.wait_ge(x_in[k % RING], 16 * (b + k // RING + 1))
                pool.tensor_tensor(y_row[:, slot(a, k), :], x_row[:, slot(a, k), :], b4_row, ALU.add).then_inc(x_b4, 1)
                pool.tensor_tensor(xb_row[:, slot(a, k), :], x_row[:, slot(a, k), :], beta_row,
                                   ALU.add).then_inc(x_beta, 1)

            add_rows(NG - 1, 0)
            pool.wait_ge(loaded_rows, 48)
            pool.wait_ge(block_done, NB * NG)
            for j in range(1, GT):
                x_plus(0, 0, j - 1)
                add_rows(NG - 1, j)
            for k in range(GT - 1, AHEAD):
                x_plus(0, 0, k)

            def mean_1(a, t, q):
                count = to_count(a + t + 1)
                pool.wait_ge(pads_set, 3)
                pool.wait_ge(y_ready, count)
                pool.tensor_scalar(nmean1[:, q], sum1[:, q], -1.0 / H, 0.0, ALU.mult, ALU.add).then_inc(nmean1_ready, 1)

            def rstd_1(a, t, q):
                count = to_count(a + t + 1)
                pool.wait_ge(pads_set, 3)
                pool.wait_ge(squared1, count)
                pool.tensor_scalar(var1[:, q], ssq1[:, q], 1.0 / H, EPS, ALU.mult, ALU.add).then_inc(var1_ready, 1)
                pool.wait_ge(var1_ready, a + t + 1)
                pool.tensor_tensor(rstd1[:, q], var1[:, q], minus_half, ALU.pow).then_inc(rstd1_ready, 1)

            def rstd_2(a, t, q):
                count = to_count(a + t + 1)
                pool.wait_ge(pads_set, 3)
                pool.wait_ge(squared2, count)
                pool.tensor_scalar(var2[:, q], ssq2[:, q], 1.0 / H, EPS, ALU.mult, ALU.add).then_inc(var2_ready, 1)
                pool.wait_ge(var2_ready, a + t + 1)
                pool.tensor_tensor(rstd2[:, q], var2[:, q], minus_half, ALU.pow).then_inc(rstd2_ready, 1)
                pool.wait_ge(nmean2_ready, a + t + 1)
                pool.wait_ge(rstd2_ready, a + t + 1)
                pool.tensor_tensor(shift2[:, q], rstd2[:, q], nmean2[:, q], ALU.mult).then_inc(shift2_ready, 1)

            def step(a, b, k, live):
                t1, t2 = k - 3, k - 4
                q, q1, q2 = (slice(t % RING, t % RING + 1) for t in (k, t1, t2))
                if live(a, t1) and over(a, k):
                    mean_1(a, t1, q1)
                if live(a, t2):
                    count = to_count(a + t2 + 1)
                    pool.wait_ge(pads_set, 3)
                    pool.wait_ge(w_ready, count)
                    pool.tensor_scalar(nmean2[:, q2], sum2[:, q2], -1.0 / H, 0.0, ALU.mult, ALU.add).then_inc(nmean2_ready, 1)
                if live(a, k) and not ahead(a, k):
                    pool.wait_ge(x_in[k % RING], 16 * (b + k // RING + 1))
                    pool.wait_ge(w_ready, a + k - RING + 1)
                    pool.tensor_tensor(y_row[:, slot(a, k), :], x_row[:, slot(a, k), :], b4_row, ALU.add).then_inc(x_b4, 1)
                if live(a, t1) and not over(a, k):
                    mean_1(a, t1, q1)
                norm_1_first = early(a, k) or over(a, k)
                if live(a, t1) and norm_1_first:
                    rstd_1(a, t1, q1)
                if live(a, t2):
                    rstd_2(a, t2, q2)
                if live(a, t1) and not norm_1_first:
                    rstd_1(a, t1, q1)
                if live(a, k) and not ahead(a, k):
                    pool.tensor_tensor(xb_row[:, slot(a, k), :], x_row[:, slot(a, k), :], beta_row,
                                       ALU.add).then_inc(x_beta, 1)

            run_steps(pool, step, 3)

        @block.tensor
        def _(pe):
            def turn_chunk(g, c):
                first, gathered = (0, src_in) if c < KC else (GT, dst_in)
                cc = c % KC
                if c == 0:
                    if past(NB * (g - 1) + KC):
                        pe.wait_ge(block_done, NB * (g - 1) + KC)
                if c == 0:
                    if past(g):
                        pe.wait_ge(eat_ready, g)
                elif c == 1:
                    if past(g - 1):
                        pe.wait_ge(same_ready, g - 1)
                    if past(XC * g):
                        pe.wait_ge(ft_split, XC * g)
                else:
                    if past(XC * g + c - 1):
                        pe.wait_ge(ft_split, XC * g + c - 1)
                for j in range(GT):
                    if cc == 0:
                        pe.wait_ge(gathered[j], 16 * (g + 1))
                    t = pe.transpose(ps[:, TURN + c % 2, j * LE:(j + 1) * LE],
                                     xg[0:LE, first + j, cc * P:(cc + 1) * P], ident[0:LE, 0:LE])
                t.then_inc(turned_x, 1)

            def turn_ea(g):
                pe.wait_ge(ea_cat_ready, g + 1)
                if past(XC * g + XC - 1):
                    pe.wait_ge(ft_split, XC * g + XC - 1)
                for j in range(GT):
                    t = pe.transpose(ps[:, TURN, j * LE:(j + 1) * LE], ea_cat[0:LE, j, :].bitcast(F32),
                                     ident[0:LE, 0:LE])
                t.then_inc(turned_ea, 1)

            def turn_dst(g):
                pe.wait_ge(dst_sum_ready, g + 1)
                if isinstance(g, int) and g == NG - 1:
                    pe.wait_ge(xt_split, 2)
                else:
                    pe.wait_ge(ft_split, XC * (g + 2))
                for j in range(GT):
                    t = pe.transpose(ps[0:LE, TURN + 1, j * LE:(j + 1) * LE],
                                     dst_sum[0:LE, j:j + 1].to_broadcast([LE, LE]), ident[0:LE, 0:LE])
                t.then_inc(turned_dst, 1)

            def w1_part(mb, c):
                split_matmul(pe, ps[:, BLOCK + mb, 0:GE], [w[:, c, mb * P:(mb + 1) * P] for w in w1],
                             [f[:, c, :] for f in ft], c == 0, False)

            def w1e_part(mb):
                cols = slice(mb * P, (mb + 1) * P)
                o = ps[:, BLOCK + mb, 0:GE]
                pe.matmul(o, w1e[0][:, cols], eat, start=False, stop=False)
                pe.matmul(o, w1e[1][0:D, cols], eat[0:D, :], start=False, stop=True).then_inc(block_done, 1)

            def w1_product(g):
                for mb in range(KC):
                    if past(NB * g + mb - KC + 1):
                        pe.wait_ge(vn_ready, NB * g + mb - KC + 1)
                    for c in range(XC):
                        if mb == 0:
                            pe.wait_ge(ft_split, XC * g + c + 1)
                        w1_part(mb, c)
                    if mb == 0:
                        pe.wait_ge(eat_ready, g + 1)
                    w1e_part(mb)

            def w2_block(g, mb):
                cols = slice(mb * P, (mb + 1) * P)
                pe.wait_ge(vn_ready, NB * g + mb + 1)
                for c in range(KC):
                    if mb == 0:
                        if isinstance(g, int) and g == 0:
                            pe.wait_ge(w_split, XC + 1 + c + 1)
                        pe.wait_ge(mish_split, NB * g + c + 1)
                    mm = split_matmul(pe, ps[:, BLOCK + mb, 0:GE], [w[:, c, cols] for w in w2],
                                      [h[:, c, :] for h in ht], c == 0, c == KC - 1)
                mm.then_inc(block_done, 1)

            def z_tile(g, j):
                if isinstance(g, int) and g == 0 and j == 0:
                    pe.wait_ge(w_split, XC + 1 + 2 * KC)
                pe.wait_ge(mish_split, NB * (g + 1))
                if z_bank(g, j) != ROWS + j % 2:
                    pe.wait_ge(vn_ready, NB * NG - KC + j + 1)
                elif past(GT * g + j - 1):
                    pe.wait_ge(agg_ready, GT * g + j - 1)
                lanes = slice(j * LE, (j + 1) * LE)
                for c in range(KC):
                    mm = split_matmul(pe, ps[0:LE, z_bank(g, j), :], [m[:, c, lanes] for m in mt],
                                      [w[:, c, :] for w in w3b], c == 0, c == KC - 1)
                mm.then_inc(z_done, 1)

            def sum_tile(g, j):
                pe.wait_ge(same_ready, g + 1)
                pe.wait_ge(z_split, GT * g + j + 1)
                o = ps[0:LE, z_bank(g, j), :]
                pe.matmul(o, same[0:LE, j, :], zs[0][0:LE, j % 2, :], start=True, stop=False)
                pe.matmul(o, same[0:LE, j, :], zs[1][0:LE, j % 2, :], start=False, stop=True).then_inc(sum_done, 1)

            def keep_warm(bank, n):
                for _ in range(n):
                    pe.matmul(ps[:, bank, 0:P], ident, ident, start=True, stop=True)

            def first_group():
                pe.wait_ge(ident_made, 2)
                keep_warm(ROWS, WARM)
                for c in range(0, XC, 2):
                    turn_chunk(0, c)
                    turn_chunk(0, c + 1)
                    pe.wait_ge(w_split, c // 2 + 1)
                    pe.wait_ge(ft_split, c // 2 + 1)
                    for mb in range(KC):
                        w1_part(mb, c // 2)
                turn_ea(0)
                for mb in range(KC):
                    for c in range(KC, XC):
                        if mb == 0:
                            pe.wait_ge(w_split, c + 1)
                            pe.wait_ge(ft_split, c + 1)
                        w1_part(mb, c)
                    if mb == 0:
                        pe.wait_ge(w_split, XC + 1)
                        pe.wait_ge(eat_ready, 1)
                    w1e_part(mb)
                turn_chunk(1, 0)
                turn_chunk(1, 1)
                keep_warm(ROWS, WARM)
                for mb in range(KC):
                    if mb < KC - 1:
                        turn_chunk(1, 2 * mb + 2)
                        turn_chunk(1, 2 * mb + 3)
                    else:
                        turn_ea(1)
                    w2_block(0, mb)

            def group(g):
                turn_dst(g - 1)
                w1_product(g)
                z_tile(g - 1, 0)
                turn_chunk(g + 1, 0)
                turn_chunk(g + 1, 1)
                z_tile(g - 1, 1)
                sum_tile(g - 1, 0)
                turn_chunk(g + 1, 2)
                turn_chunk(g + 1, 3)
                z_tile(g - 1, 2)
                sum_tile(g - 1, 1)
                turn_chunk(g + 1, 4)
                turn_chunk(g + 1, 5)
                z_tile(g - 1, 3)
                sum_tile(g - 1, 2)
                turn_chunk(g + 1, 6)
                turn_chunk(g + 1, 7)
                w2_block(g, 0)
                sum_tile(g - 1, 3)
                turn_ea(g + 1)
                for mb in range(1, KC):
                    w2_block(g, mb)

            def last_group():
                g = NG - 1
                turn_dst(g - 1)
                w1_product(g)
                pe.wait_ge(eat_ready, NG)
                z_tile(g - 1, 0)
                z_tile(g - 1, 1)
                turn_x(0, 0, 0)
                turn_x(0, 0, 1)
                w2_block(g, 0)
                sum_tile(g - 1, 0)
                sum_tile(g - 1, 1)
                w2_block(g, 1)
                z_tile(g - 1, 2)
                z_tile(g - 1, 3)
                w2_block(g, 2)
                w2_block(g, 3)
                sum_tile(g - 1, 2)
                sum_tile(g - 1, 3)

            def last_rows():
                g = NG - 1
                turn_dst(g)
                w3_product(0, 0, 0)
                w3_product(0, 0, 1)
                z_tile(g, 0)
                z_tile(g, 1)
                sum_tile(g, 0)
                z_tile(g, 2)
                sum_tile(g, 1)
                z_tile(g, 3)
                sum_tile(g, 2)
                turn_x(0, 0, 2)
                turn_x(0, 0, 3)
                sum_tile(g, 3)
                w3_product(0, 0, 2)
                turn_x(0, 0, 4)
                w3_product(0, 0, 3)
                turn_x(0, 0, 5)
                w3_product(0, 0, 4)
                w3_product(0, 0, 5)
                keep_warm(TURN, WARM * 2 // 3)

            def turn_x(a, b, k):
                pe.wait_ge(x_in[k % RING], 16 * (b + k // RING + 1))
                if past(a + k - 1):
                    pe.wait_ge(xt_split, a + k - 1)
                if isinstance(a, int) and a + k in (1, 3):
                    pe.wait_ge(same_ready, NG - 1 if a + k == 1 else NG)
                for c in range(KC):
                    t = pe.transpose(ps[:, TURN + k % 2, c * P:(c + 1) * P],
                                     x_row[:, slot(a, k), c * P:(c + 1) * P], ident)
                t.then_inc(turned_node, 1)

            def turn_u(a, b, k):
                pe.wait_ge(mish_ready, NB * NG + a + k + 1)
                if isinstance(a, int) and a + k < 2:
                    pe.wait_ge(v_ready, a + k + 3)
                else:
                    pe.wait_ge(ut_split, a + k - 1)
                for c in range(KC):
                    t = pe.transpose(ps[:, BLOCK + 2 + k % 2, c * P:(c + 1) * P],
                                     f_buf[:, k % 2, c * P:(c + 1) * P], ident)
                t.then_inc(turned_u, 1)

            def w3_product(a, b, k):
                if isinstance(a, int) and a + k == 0:
                    pe.wait_ge(w_split, XC + 1 + 3 * KC)
                pe.wait_ge(xt_split, a + k + 1)
                if not ahead(a, k):
                    pe.wait_ge(v_ready, a + k - 1)
                elif k < 2:
                    pe.wait_ge(vn_ready, NB * NG - KC + k + 1)
                else:
                    pe.wait_ge(agg_ready, GT * (NG - 1) + (k + 1 if k < 4 else GT))
                for c in range(KC):
                    mm = split_matmul(pe, ps[:, w3_bank(a, k), :], [v[:, k % 2, c, :] for v in xt],
                                      [w[:, c, :] for w in w3a], c == 0, c == KC - 1)
                mm.then_inc(w3_done, 1)

            def w4_product(a, b, k):
                if isinstance(a, int) and a + k == 0:
                    pe.wait_ge(w_split, XC + 1 + 4 * KC)
                pe.wait_ge(ut_split, a + k + 1)
                if isinstance(a, int) and a + k < 2:
                    pe.wait_ge(v_ready, a + k + 5)
                else:
                    pe.wait_ge(y_ready, a + k - 1)
                for c in range(KC):
                    mm = split_matmul(pe, ps[:, ROWS + k % 2, :], [v[:, k % 2, c, :] for v in ut],
                                      [w[:, c, :] for w in w4], c == 0, c == KC - 1)
                mm.then_inc(w4_done, 1)

            def step(a, b, k, live):
                if live(a, k + 2) and not ahead(a, k + 2):
                    turn_x(a, b, k + 2)
                u_first = early(a, k) and k < 5
                if u_first:
                    turn_u(a, b, k - 2)
                if live(a, k - 3) and not lone(a, k, 3):
                    w4_product(a, b, k - 3)
                if lone(a, k, 2):
                    w4_product(a, b, k - 2)
                if live(a, k - 2) and not u_first and not lone(a, k, 2):
                    turn_u(a, b, k - 2)
                if lone(a, k, 1):
                    turn_u(a, b, k - 1)
                if live(a, k + 1) and not ahead(a, k + 1):
                    w3_product(a, b, k + 1)

            first_group()
            group(1)
            with pe.Fori(2, NG - 1) as g:
                group(g)
            last_group()
            last_rows()
            run_steps(pe, step, 2)

        @block.scalar
        def _(act):
            def weight_hi(out_, in_):
                act.activation(out_, in_, ACT.Copy).then_inc(w_hi_ready, 1)

            def mish_exp(g, b):
                i = NB * g + b
                act.wait_ge(block_done, i + 1)
                if past(i - 1):
                    act.wait_ge(mish_ready, i - 1)
                act.activation(e_buf[:, b % 2, 0:GE], ps[:, BLOCK + b % KC, 0:GE], ACT.Exp,
                               bias=(b1_col if b < KC else b2_col)[:, b % KC:b % KC + 1]).then_inc(e_ready, 1)

            def mish_inverse(slot, width, i):
                act.wait_ge(n_ready, i + 1)
                act.activation(e_buf[:, slot, 0:width], n_buf[:, slot, 0:width], ACT.Ln, bias=2.0).then_inc(ln_done, 1)
                act.wait_ge(ln_done, i + 1)
                act.activation(e_buf[:, slot, 0:width], e_buf[:, slot, 0:width], ACT.Exp, scale=-1.0).then_inc(inv_ready, 1)

            def mish_hi(g, b):
                i = NB * g + b
                act.wait_ge(mish_ready, i + 1)
                if b < KC:
                    if past(NB * g):
                        act.wait_ge(block_done, NB * g)
                else:
                    if past(GT * g):
                        act.wait_ge(z_done, GT * g)
                act.activation((ht if b < KC else mt)[0][:, b % KC, :], f_buf[:, b % 2, 0:GE], ACT.Copy).then_inc(mish_hi_ready, 1)

            def mish_blocks(g, first_block, before_last=None, after_exp=None):
                n = KC
                mish_exp(g, first_block)
                if after_exp:
                    after_exp(first_block)
                for b in range(first_block, first_block + n):
                    mish_inverse(b % 2, GE, NB * g + b)
                    if b + 1 < first_block + n:
                        mish_exp(g, b + 1)
                        if after_exp:
                            after_exp(b + 1)
                    elif before_last:
                        before_last()
                    mish_hi(g, b)

            def ft_hi(g, c):
                act.wait_ge(turned_x, XC * g + c + 1)
                if c == 0:
                    if past(NB * (g - 1) + KC):
                        act.wait_ge(block_done, NB * (g - 1) + KC)
                act.activation(ft[0][:, c, :], ps[:, TURN + c % 2, 0:GE], ACT.Copy).then_inc(ft_hi_ready, 1)

            def z_hi(g, j):
                act.wait_ge(z_done, GT * g + j + 1)
                if past(GT * g + j - 1):
                    act.wait_ge(sum_done, GT * g + j - 1)
                act.activation(zs[0][0:LE, j % 2, :], ps[0:LE, z_bank(g, j), :], ACT.Copy).then_inc(z_hi_ready, 1)

            def agg_out(g, j):
                act.wait_ge(sum_done, GT * g + j + 1)
                if past(16 * (GT * (g - 1) + j + 1)):
                    act.wait_ge(added, 16 * (GT * (g - 1) + j + 1))
                act.activation(agg[0:LE, j, :], ps[0:LE, z_bank(g, j), :], ACT.Copy).then_inc(agg_ready, 1)

            def first_group():
                def more(b):
                    for c in (2 * (b - KC) + 4, 2 * (b - KC) + 5):
                        if c < XC:
                            ft_hi(1, c)

                mish_blocks(0, 0, before_last=lambda: ft_hi(1, 0))
                for c in range(1, 4):
                    ft_hi(1, c)
                act.wait_ge(loaded_w3b, 16)
                for c in range(KC):
                    weight_hi(w3b[0][:, c, :], w3b_in[:, c, :])
                act.wait_ge(w_split, XC + 1 + 2 * KC)
                mish_blocks(0, KC, after_exp=more)

            def group(g):
                def before_last():
                    z_hi(g - 1, 0)
                    ft_hi(g + 1, 0)

                mish_blocks(g, 0, before_last=before_last)
                ft_hi(g + 1, 1)
                z_hi(g - 1, 1)
                agg_out(g - 1, 0)
                ft_hi(g + 1, 2)
                ft_hi(g + 1, 3)
                z_hi(g - 1, 2)
                agg_out(g - 1, 1)
                ft_hi(g + 1, 4)
                ft_hi(g + 1, 5)
                z_hi(g - 1, 3)
                agg_out(g - 1, 2)
                ft_hi(g + 1, 6)
                ft_hi(g + 1, 7)
                agg_out(g - 1, 3)
                mish_blocks(g, KC)

            def last_group():
                g = NG - 1
                mish_blocks(g, 0, before_last=lambda: z_hi(g - 1, 0))
                z_hi(g - 1, 1)
                xt_hi(0, 0, 0)
                xt_hi(0, 0, 1)
                act.wait_ge(loaded_w3a, 16)
                for c in range(KC):
                    weight_hi(w3a[0][:, c, :], w34_in[:, c, :])
                mish_exp(g, KC)
                agg_out(g - 1, 0)
                agg_out(g - 1, 1)
                mish_inverse(KC % 2, GE, NB * g + KC)
                mish_exp(g, KC + 1)
                mish_hi(g, KC)
                mish_inverse((KC + 1) % 2, GE, NB * g + KC + 1)
                mish_hi(g, KC + 1)
                z_hi(g - 1, 2)
                z_hi(g - 1, 3)
                mish_exp(g, KC + 2)
                mish_inverse((KC + 2) % 2, GE, NB * g + KC + 2)
                mish_exp(g, KC + 3)
                mish_hi(g, KC + 2)
                agg_out(g - 1, 2)
                agg_out(g - 1, 3)
                mish_inverse((KC + 3) % 2, GE, NB * g + KC + 3)
                mish_hi(g, KC + 3)

            def last_rows():
                g = NG - 1
                z_hi(g, 0)
                z_hi(g, 1)
                agg_out(g, 0)
                z_hi(g, 2)
                agg_out(g, 1)
                z_hi(g, 3)
                agg_out(g, 2)
                xt_hi(0, 0, 2)
                xt_hi(0, 0, 3)
                agg_out(g, 3)
                xt_hi(0, 0, 4)
                xt_hi(0, 0, 5)
                act.wait_ge(loaded_w4, 16)
                for c in range(KC):
                    weight_hi(w4[0][:, c, :], w34_in[:, KC + c, :])

            act.preload_act_table_set("natural_log_exp_and_others")
            act.wait_ge(loaded_w1a, 16)
            for c in range(KC):
                weight_hi(w1[0][:, c, :], w1_in[:, c, :])
            for c in range(KC):
                ft_hi(0, c)
            act.wait_ge(loaded_w1b, 16)
            for c in range(KC, XC):
                weight_hi(w1[0][:, c, :], w1_in[:, c, :])
            for c in range(KC, XC - 2):
                ft_hi(0, c)
            act.wait_ge(loaded_w1e, 32)
            weight_hi(w1e[0], w1e_in)
            for c in range(XC - 2, XC):
                ft_hi(0, c)
            act.wait_ge(loaded_w2, 16)
            for c in range(KC):
                weight_hi(w2[0][:, c, :], w2_in[:, c, :])
            act.wait_ge(loaded_bias, 32)
            act.wait_ge(constants_made, 5)
            act.wait_ge(w_split, XC + 1 + KC)

            M0 = NB * NG

            def xt_hi(a, b, k):
                act.wait_ge(turned_node, a + k + 1)
                if past(a + k - 1):
                    act.wait_ge(w3_done, a + k - 1)
                act.activation(xt[0][:, k % 2].rearrange("p c n -> p (c n)"), ps[:, TURN + k % 2, :],
                               ACT.Copy).then_inc(xt_hi_ready, 1)

            def ut_hi(a, b, k):
                act.wait_ge(turned_u, a + k + 1)
                if past(a + k - 1):
                    act.wait_ge(w4_done, a + k - 1)
                act.activation(ut[0][:, k % 2].rearrange("p c n -> p (c n)"), ps[:, BLOCK + 2 + k % 2, :],
                               ACT.Copy).then_inc(ut_hi_ready, 1)

            def node_exp(a, b, k):
                act.wait_ge(v_ready, a + k + 1)
                act.wait_ge(mish_ready, M0 + a + k - 1)
                act.activation(e_buf[:, k % 2, :], v_row[:, slot(a, k), :], ACT.Exp).then_inc(e_ready, 1)

            def node_square(a, b, k):
                act.wait_ge(e_held, M0 + a + k + 1)
                act.wait_ge(mish_ready, M0 + a + k - 1)
                act.activation(n_buf[:, k % 2, :], e_buf[:, k % 2, :], ACT.Square).then_inc(n_ready, 1)

            def node_ln(a, b, k):
                act.wait_ge(n_ready, M0 + a + k + 1)
                act.activation(e_buf[:, k % 2, :], n_buf[:, k % 2, :], ACT.Ln, bias=1.0).then_inc(ln_done, 1)

            def node_inverse(a, b, k):
                act.wait_ge(ln_done, M0 + a + k + 1)
                act.activation(e_buf[:, k % 2, :], e_buf[:, k % 2, :], ACT.Exp, scale=-1.0).then_inc(inv_ready, 1)

            def squares_y(a, b, k):
                q = k % RING
                act.wait_ge(nmean1_ready, a + k + 1)
                if past(a + k):
                    act.wait_ge(squared1, a + k)
                act.activation(unused[:, 0, :], y_row[:, slot(a, k), :], ACT.Square, bias=nmean1[:, q:q + 1],
                               accum_out=ssq1[:, q:q + 1]).then_inc(squared1, 1)

            def squares_w(a, b, k):
                q = k % RING
                act.wait_ge(nmean2_ready, a + k + 1)
                if past(a + k):
                    act.wait_ge(squared2, a + k)
                act.activation(unused[:, 1, :], w_row[:, k % 2, :], ACT.Square, bias=nmean2[:, q:q + 1],
                               accum_out=ssq2[:, q:q + 1]).then_inc(squared2, 1)

            def final(a, b, k):
                q = k % RING
                act.wait_ge(shift2_ready, a + k + 1)
                if past(16 * (b + k // RING)):
                    act.wait_ge(stored[q], 16 * (b + k // RING))
                act.activation(o_row[:, q, :], w_row[:, k % 2, :], ACT.Identity, bias=shift2[:, q:q + 1],
                               scale=rstd2[:, q:q + 1]).then_inc(normed, 1)

            def step(a, b, k, live):
                if early(a, k):
                    node_exp(a, b, k - 1)
                    if k == 5:
                        xt_hi(a, b, 7)
                    node_square(a, b, k - 1)
                    if k == 5:
                        squares_y(a, b, 1)
                    node_ln(a, b, k - 1)
                    if k == 4:
                        ut_hi(a, b, 2)
                    if k == 5:
                        squares_w(a, b, 0)
                    node_inverse(a, b, k - 1)
                    if k == 4:
                        squares_y(a, b, 0)
                        xt_hi(a, b, 6)
                    if k == 5:
                        ut_hi(a, b, 3)
                        squares_y(a, b, 2)
                    return
                if isinstance(a, int) and k == AHEAD + 1:
                    final(a, b, 1)
                if isinstance(a, int) and k == AHEAD:
                    final(a, b, 0)
                elif lone(a, k, 1):
                    ut_hi(a, b, k - 2)
                    final(a, b, k - 5)
                elif live(a, k - 5) and not early(a, k):
                    final(a, b, k - 5)
                if lone(a, k, 0):
                    node_exp(a, b, k - 1)
                    node_exp(a, b, k)
                    node_square(a, b, k - 1)
                    node_ln(a, b, k - 1)
                    node_square(a, b, k)
                    ut_hi(a, b, k - 2)
                    node_inverse(a, b, k - 1)
                    node_ln(a, b, k)
                    node_inverse(a, b, k)
                    squares_y(a, b, k - 3)
                    squares_w(a, b, k - 4)
                    return
                if lone(a, k, 1):
                    ut_hi(a, b, k - 1)
                    squares_y(a, b, k - 3)
                    squares_w(a, b, k - 4)
                    return
                if live(a, k - 1):
                    node_exp(a, b, k - 1)
                if live(a, k + 2):
                    xt_hi(a, b, k + 2)
                if live(a, k - 1):
                    node_square(a, b, k - 1)
                    node_ln(a, b, k - 1)
                after_early = isinstance(a, int) and k == AHEAD
                if after_early:
                    squares_w(a, b, 1)
                elif live(a, k - 4) and not over(a, k):
                    squares_w(a, b, k - 4)
                if live(a, k - 1):
                    node_inverse(a, b, k - 1)
                if live(a, k - 2) and not over(a, k):
                    ut_hi(a, b, k - 2)
                if after_early:
                    squares_w(a, b, k - 4)
                if live(a, k - 3):
                    squares_y(a, b, k - 3)
                if live(a, k - 4) and over(a, k):
                    squares_w(a, b, k - 4)

            first_group()
            group(1)
            with act.Fori(2, NG - 1) as g:
                group(g)
            last_group()
            last_rows()
            node_exp(0, 0, 0)
            node_exp(0, 0, 1)
            for k in range(2):
                node_square(0, 0, k)
                node_ln(0, 0, k)
                node_inverse(0, 0, k)
            ut_hi(0, 0, 0)
            ut_hi(0, 0, 1)
            run_steps(act, step, 3)

        @block.vector
        def _(dve):
            def weight_lo(i, out_, in_, hi):
                dve.wait_ge(w_hi_ready, i + 1)
                dve.tensor_tensor(out_, in_, hi.bitcast(F32), ALU.subtract).then_inc(w_split, 1)

            def mish_n(slot, width, i):
                e = e_buf[:, slot, 0:width]
                dve.wait_ge(e_ready, i + 1)
                dve.tensor_scalar(e, e, E_MAX, None, ALU.min).then_inc(e_held, 1)
                dve.wait_ge(e_held, i + 1)
                if past(i - 1):
                    dve.wait_ge(mish_ready, i - 1)
                dve.scalar_tensor_tensor(out=n_buf[:, slot, 0:width], in0=e, scalar=2.0, in1=e,
                                         op0=ALU.add, op1=ALU.mult).then_inc(n_ready, 1)

            def block_vn(g, b):
                i = NB * g + b
                bias = (b1_col if b < KC else b2_col)[:, b % KC:b % KC + 1]
                dve.wait_ge(n_ready, i + 1)
                dve.wait_ge(ln_done, i + 1)
                dve.scalar_tensor_tensor(out=n_buf[:, b % 2, 0:GE], in0=ps[:, BLOCK + b % KC, 0:GE], scalar=bias,
                                         in1=n_buf[:, b % 2, 0:GE], op0=ALU.add, op1=ALU.mult).then_inc(vn_ready, 1)

            def mish_f(slot, width, i):
                dve.wait_ge(inv_ready, i + 1)
                dve.wait_ge(vn_ready, i + 1)
                dve.tensor_tensor(f_buf[:, slot, 0:width], n_buf[:, slot, 0:width], e_buf[:, slot, 0:width],
                                  ALU.mult).then_inc(mish_ready, 1)

            def block_lo(g, b):
                i = NB * g + b
                t = ht if b < KC else mt
                dve.wait_ge(mish_hi_ready, i + 1)
                dve.tensor_tensor(t[1][:, b % KC, :], f_buf[:, b % 2, 0:GE], t[0][:, b % KC, :].bitcast(F32),
                                  ALU.subtract).then_inc(mish_split, 1)

            def mish_blocks(g, first_block, n=KC, before_last=None, after_n=None):
                for b in range(first_block, first_block + n):
                    mish_n(b % 2, GE, NB * g + b)
                    if b > first_block:
                        block_lo(g, b - 1)
                    if after_n:
                        after_n(b)
                    block_vn(g, b)
                    if past(NB * g + b - 1):
                        mish_split_before = NB * g + b - 1
                        dve.wait_ge(mish_hi_ready, mish_split_before)
                        dve.wait_ge(mish_split, mish_split_before)
                    mish_f(b % 2, GE, NB * g + b)
                if before_last:
                    before_last()
                block_lo(g, first_block + n - 1)

            def ft_lo(g, c):
                dve.wait_ge(ft_hi_ready, XC * g + c + 1)
                dve.tensor_tensor(ft[1][:, c, :], ps[:, TURN + c % 2, 0:GE], ft[0][:, c, :].bitcast(F32),
                                  ALU.subtract).then_inc(ft_split, 1)

            def ea_out(g):
                dve.wait_ge(turned_ea, g + 1)
                dve.tensor_copy(eat, ps[:, TURN, 0:GE]).then_inc(eat_ready, 1)

            def ea_split(g):
                rows = ea_all[0:LE, bass.ds(g * GT, GT), :]
                if past(g):
                    dve.wait_ge(turned_ea, g)
                dve.tensor_copy(ea_cat[0:LE, :, 0:D], rows).then_inc(ea_hi_ready, 1)
                dve.wait_ge(ea_hi_ready, g + 1)
                dve.tensor_tensor(ea_cat[0:LE, :, D:2 * D], rows, ea_cat[0:LE, :, 0:D].bitcast(F32),
                                  ALU.subtract).then_inc(ea_cat_ready, 1)

            def z_lo(g, j):
                dve.wait_ge(z_hi_ready, GT * g + j + 1)
                dve.tensor_tensor(zs[1][0:LE, j % 2, :], ps[0:LE, z_bank(g, j), :], zs[0][0:LE, j % 2, :].bitcast(F32),
                                  ALU.subtract).then_inc(z_split, 1)

            def same_dst(g):
                dve.wait_ge(turned_dst, g + 1)
                if past(GT * g):
                    dve.wait_ge(sum_done, GT * g)
                for j in range(GT):
                    dve.tensor_scalar(same[0:LE, j, :], ps[0:LE, TURN + 1, j * LE:(j + 1) * LE],
                                      dst_sum[0:LE, j:j + 1], None, ALU.is_equal).then_inc(same_part_ready, 1)
                dve.wait_ge(same_part_ready, GT * (g + 1))
                dve.tensor_tensor(same_below[0:LE], same[0:LE].bitcast(F32),
                                  below[0:LE].rearrange("p (a n) -> p a n", a=1).to_broadcast([LE, GT, LE]),
                                  ALU.mult).then_inc(same_ready, 1)
                dve.wait_ge(same_ready, g + 1)
                dve.tensor_reduce(n_before[0:LE, :], same_below[0:LE], AX.X, ALU.add).then_inc(counted, 1)
                if past(g):
                    dve.wait_ge(add_row_ready, g)
                dve.tensor_scalar(to_unread, dst_sum, unread_f, -1.0, ALU.subtract, ALU.mult).then_inc(distance, 1)
                dve.wait_ge(counted, g + 1)
                dve.wait_ge(distance, g + 1)
                dve.scalar_tensor_tensor(out=to_unread, in0=n_before, scalar=1.0, in1=to_unread, op0=ALU.min,
                                         op1=ALU.mult).then_inc(moved, 1)
                dve.wait_ge(moved, g + 1)
                if past(16 * GT * g):
                    dve.wait_ge(added, 16 * GT * g)
                dve.tensor_tensor(add_row, to_unread, dst_sum, ALU.add).then_inc(add_row_ready, 1)

            def take_dst(g):
                if past(g):
                    dve.wait_ge(add_row_ready, g)
                dve.tensor_copy(dst_sum, dst_f[:, bass.ds(g * GT, GT)]).then_inc(dst_sum_ready, 1)

            def first_group():
                def more(b):
                    for c in (2 * (b - KC) + 4, 2 * (b - KC) + 5):
                        if c < XC:
                            ft_lo(1, c)

                take_dst(0)
                mish_blocks(0, 0, before_last=lambda: ft_lo(1, 0))
                for c in range(1, 4):
                    ft_lo(1, c)
                dve.wait_ge(loaded_ea_rest, 16)
                ea_split(1)
                for c in range(KC):
                    weight_lo(XC + 1 + KC + c, w3b[1][:, c, :], w3b_in[:, c, :], w3b[0][:, c, :])
                mish_blocks(0, KC, after_n=more)
                ea_out(1)

            def group(g):
                def before_last():
                    z_lo(g - 1, 0)
                    ft_lo(g + 1, 0)

                same_dst(g - 1)
                take_dst(g)
                ea_split(g + 1)
                mish_blocks(g, 0, before_last=before_last)
                ft_lo(g + 1, 1)
                z_lo(g - 1, 1)
                ft_lo(g + 1, 2)
                ft_lo(g + 1, 3)
                z_lo(g - 1, 2)
                ft_lo(g + 1, 4)
                ft_lo(g + 1, 5)
                z_lo(g - 1, 3)
                ft_lo(g + 1, 6)
                ft_lo(g + 1, 7)
                ea_out(g + 1)
                mish_blocks(g, KC)

            def last_group():
                g = NG - 1
                same_dst(g - 1)
                take_dst(g)
                mish_blocks(g, 0, before_last=lambda: z_lo(g - 1, 0))
                z_lo(g - 1, 1)
                xt_lo(0, 0, 0)
                xt_lo(0, 0, 1)
                for c in range(KC):
                    weight_lo(XC + 1 + 2 * KC + c, w3a[1][:, c, :], w34_in[:, c, :], w3a[0][:, c, :])
                mish_blocks(g, KC, 2)
                z_lo(g - 1, 2)
                z_lo(g - 1, 3)
                mish_blocks(g, KC + 2, 2)

            def last_rows():
                g = NG - 1
                same_dst(g)
                for j in range(GT):
                    z_lo(g, j)
                for k in range(2, AHEAD):
                    xt_lo(0, 0, k)
                for c in range(KC):
                    weight_lo(XC + 1 + 3 * KC + c, w4[1][:, c, :], w34_in[:, KC + c, :], w4[0][:, c, :])

            def w1_lo(c):
                weight_lo(c, w1[1][:, c, :], w1_in[:, c, :], w1[0][:, c, :])

            for c in range(KC):
                w1_lo(c)
            dve.wait_ge(loaded_ea_first, 16)
            ea_split(0)
            for c in range(KC):
                ft_lo(0, c)
            for c in range(KC, XC):
                w1_lo(c)
            for c in range(KC, XC - 2):
                ft_lo(0, c)
            weight_lo(XC, w1e[1], w1e_in, w1e[0])
            for c in range(XC - 2, XC):
                ft_lo(0, c)
            ea_out(0)
            for c in range(KC):
                weight_lo(XC + 1 + c, w2[1][:, c, :], w2_in[:, c, :], w2[0][:, c, :])
            dve.wait_ge(loaded_pad, 16)
            dve.wait_ge(unread_set, 1)
            dve.tensor_copy(dst_f, dst_pad).then_inc(dst_float, 1)
            dve.tensor_copy(unread_f, unread_i).then_inc(dst_float, 1)
            dve.wait_ge(loaded_bias, 32)
            dve.wait_ge(dst_float, 2)
            dve.wait_ge(constants_made, 5)

            M0 = NB * NG

            def xt_lo(a, b, k):
                dve.wait_ge(xt_hi_ready, a + k + 1)
                dve.tensor_tensor(xt[1][:, k % 2].rearrange("p c n -> p (c n)"), ps[:, TURN + k % 2, :],
                                  xt[0][:, k % 2].rearrange("p c n -> p (c n)").bitcast(F32),
                                  ALU.subtract).then_inc(xt_split, 1)

            def ut_lo(a, b, k):
                dve.wait_ge(ut_hi_ready, a + k + 1)
                dve.tensor_tensor(ut[1][:, k % 2].rearrange("p c n -> p (c n)"), ps[:, BLOCK + 2 + k % 2, :],
                                  ut[0][:, k % 2].rearrange("p c n -> p (c n)").bitcast(F32),
                                  ALU.subtract).then_inc(ut_split, 1)

            def add_pre(a, b, k):
                q = k % RING
                dve.wait_ge(w3_done, a + k + 1)
                dve.wait_ge(pre_in[q], 16 * (b + k // RING + 1))
                v = v_row[:, slot(a, k), :]
                dve.tensor_tensor(v, ps[:, w3_bank(a, k), :], v, ALU.add).then_inc(v_ready, 1)

            def node_held(a, b, k):
                e = e_buf[:, k % 2, :]
                dve.wait_ge(e_ready, M0 + a + k + 1)
                dve.tensor_scalar(e, e, E_MAX, 1.0, ALU.min, ALU.add).then_inc(e_held, 1)

            def node_vn(a, b, k):
                v = v_row[:, slot(a, k), :]
                dve.wait_ge(n_ready, M0 + a + k + 1)
                dve.scalar_tensor_tensor(out=v, in0=n_buf[:, k % 2, :], scalar=-1.0, in1=v,
                                         op0=ALU.add, op1=ALU.mult).then_inc(vn_ready, 1)

            def node_f(a, b, k):
                dve.wait_ge(inv_ready, M0 + a + k + 1)
                dve.wait_ge(vn_ready, M0 + a + k + 1)
                if past(a + k - 1):
                    dve.wait_ge(turned_u, a + k - 1)
                dve.tensor_tensor(f_buf[:, k % 2, :], v_row[:, slot(a, k), :], e_buf[:, k % 2, :],
                                  ALU.mult).then_inc(mish_ready, 1)

            def residual(a, b, k):
                q = k % RING
                dve.wait_ge(w4_done, a + k + 1)
                dve.wait_ge(x_b4, a + k + 1)
                dve.scalar_tensor_tensor(out=y_row[:, slot(a, k), :], in0=ps[:, ROWS + k % 2, :], scalar=1.0, in1=y_row[:, slot(a, k), :],
                                         op0=ALU.mult, op1=ALU.add,
                                         accum_out=sum1[:, q:q + 1]).then_inc(y_ready, 1)

            def norm_gamma(a, b, k):
                q = k % RING
                dve.wait_ge(nmean1_ready, a + k + 1)
                dve.wait_ge(squared1, a + k + 1)
                dve.scalar_tensor_tensor(out=y_row[:, slot(a, k), :], in0=y_row[:, slot(a, k), :], scalar=nmean1[:, q:q + 1],
                                         in1=gamma_row, op0=ALU.add, op1=ALU.mult).then_inc(y_gamma_ready, 1)

            def residual2(a, b, k):
                q = k % RING
                dve.wait_ge(rstd1_ready, a + k + 1)
                if past(a + k - 1):
                    dve.wait_ge(normed, a + k - 1)
                dve.wait_ge(y_gamma_ready, a + k + 1)
                dve.wait_ge(x_beta, a + k + 1)
                dve.scalar_tensor_tensor(out=w_row[:, k % 2, :], in0=y_row[:, slot(a, k), :], scalar=rstd1[:, q:q + 1],
                                         in1=xb_row[:, slot(a, k), :], op0=ALU.mult, op1=ALU.add,
                                         accum_out=sum2[:, q:q + 1]).then_inc(w_ready, 1)

            def step(a, b, k, live):
                if early(a, k):
                    node_held(a, b, k - 1)
                    node_vn(a, b, k - 1)
                    if k == 4:
                        ut_lo(a, b, 2)
                    if k == 5:
                        residual(a, b, 2)
                    node_f(a, b, k - 1)
                    if k == 5:
                        ut_lo(a, b, 3)
                    if k >= 4:
                        xt_lo(a, b, k + 2)
                        norm_gamma(a, b, k - 4)
                    if k <= 4:
                        residual(a, b, k - 3)
                    if k >= 4:
                        residual2(a, b, k - 4)
                    return
                if lone(a, k, 0):
                    add_pre(a, b, k - 1)
                    add_pre(a, b, k)
                    norm_gamma(a, b, k - 4)
                    node_held(a, b, k - 1)
                    residual2(a, b, k - 4)
                    node_held(a, b, k)
                    node_vn(a, b, k - 1)
                    residual(a, b, k - 3)
                    ut_lo(a, b, k - 2)
                    node_f(a, b, k - 1)
                    node_vn(a, b, k)
                    node_f(a, b, k)
                    return
                if lone(a, k, 1):
                    norm_gamma(a, b, k - 4)
                    ut_lo(a, b, k - 2)
                    residual2(a, b, k - 4)
                    residual(a, b, k - 3)
                    ut_lo(a, b, k - 1)
                    return
                if live(a, k - 1) and not ahead(a, k - 1):
                    add_pre(a, b, k - 1)
                if live(a, k - 4):
                    norm_gamma(a, b, k - 4)
                if live(a, k - 1):
                    node_held(a, b, k - 1)
                if live(a, k - 4) and not over(a, k):
                    residual2(a, b, k - 4)
                if live(a, k + 2):
                    xt_lo(a, b, k + 2)
                if live(a, k - 3):
                    residual(a, b, k - 3)
                if live(a, k - 4) and over(a, k):
                    residual2(a, b, k - 4)
                if live(a, k - 1):
                    node_vn(a, b, k - 1)
                    node_f(a, b, k - 1)
                if live(a, k - 2) and not over(a, k):
                    ut_lo(a, b, k - 2)

            first_group()
            group(1)
            with dve.Fori(2, NG - 1) as g:
                group(g)
            last_group()
            last_rows()
            dve.wait_ge(loaded_rows, 48)
            dve.wait_ge(mish_hi_ready, M0)
            dve.wait_ge(mish_split, M0)
            add_pre(0, 0, 0)
            add_pre(0, 0, 1)
            node_held(0, 0, 0)
            add_pre(0, 0, 2)
            node_vn(0, 0, 0)
            node_held(0, 0, 1)
            add_pre(0, 0, 3)
            node_f(0, 0, 0)
            node_vn(0, 0, 1)
            add_pre(0, 0, 4)
            node_f(0, 0, 1)
            add_pre(0, 0, 5)
            ut_lo(0, 0, 0)
            ut_lo(0, 0, 1)
            run_steps(dve, step, 3)


_INS = ["x", "src", "dst", "edge_attr_64"] + [
    f"L0_gnn_{n}" for n in ("W1", "b1", "W2", "b2", "W3", "b3", "W4", "b4", "gamma", "beta")]


def kernel(**inputs):
    import numpy as np
    import concourse.bacc as bacc
    from concourse.bass_utils import run_bass_kernel_spmd

    nc = bacc.Bacc("TRN2", target_bir_lowering=False, num_devices=1)
    arrays, args = {}, []
    for name in _INS:
        a = np.ascontiguousarray(inputs[name])
        arrays[f"in_{name}"] = a
        args.append(nc.dram_tensor(f"in_{name}", a.shape, mybir.dt.from_np(a.dtype), kind="ExternalInput").ap())
    out = nc.dram_tensor("out_rows", inputs["x"].shape, F32, kind="ExternalOutput").ap()
    gnn_kernel(nc, *args, out)
    r = run_bass_kernel_spmd(nc, [arrays], core_ids=[0])
    return r.results[0]["out_rows"]
```
